# Optimizing a Trainium2 kernel written in Bass

```python
import numpy as np
import jax
import jax.numpy as jnp

def _softmax(x, axis=-1):
    return jax.nn.softmax(x, axis=axis)

def _gelu(x):
    return jax.nn.gelu(x, approximate=True)

def _silu(x):
    return jax.nn.silu(x)

def _sigmoid(x):
    return jax.nn.sigmoid(x)

def _layernorm(x, axis=-1, eps=1e-05):
    m = jnp.mean(x, axis=axis, keepdims=True)
    v = jnp.var(x, axis=axis, keepdims=True)
    return (x - m) / jnp.sqrt(v + eps)

def _scatter_add(tgt, idx, src, axis=0):
    return tgt.at[idx].add(src)

def _segment_sum(src, seg, n):
    return jax.ops.segment_sum(src, seg, n)
kernel_name = 'mk_gnn_preln_d2_gnn_r64_e68f54'

def setup_inputs(seed: int=0):
    np.random.seed(seed)
    _w = jnp.asarray

    def _rec_inputs():
        import jax
        import jax.numpy as jnp
        _gk = jax.random.key(seed)
        x = -0.000202 + 1 * jax.random.normal(jax.random.fold_in(_gk, 1), (100000, 128), jnp.float32)
        src = jax.random.randint(jax.random.fold_in(_gk, 2), (50000,), 0, 100000, jnp.int32)
        dst = jax.random.randint(jax.random.fold_in(_gk, 3), (50000,), 0, 100000, jnp.int32)
        _o = jnp.argsort(dst, stable=True)
        src = src[_o]
        dst = dst[_o]
        return (x, src, dst)
    x, src, dst = _rec_inputs()

    def _L0_gnn_setup():
        import jax, jax.numpy as jnp
        import numpy as np
        N_NODES = 50000
        N_EDGES = 12500
        D_IN = 128
        D_HID = 256
        D_OUT = 128

        def _gin_conv(x, edge_index, Wa, ba, Wb, bb):
            src, dst = (edge_index[0], edge_index[1])
            agg = jax.ops.segment_sum(x[src], dst, num_segments=x.shape[0])
            h = x + agg
            h = jnp.maximum(h @ Wa + ba, 0.0)
            return h @ Wb + bb
        key = jax.random.key(seed)
        ks = jax.random.split(key, 10)
        x = jax.random.normal(ks[0], (N_NODES, D_IN), dtype=jnp.float32)
        edge_index = jax.random.randint(ks[1], (2, N_EDGES), 0, N_NODES, dtype=jnp.int64)

        def lin(k, fan_in, fan_out):
            bound = 1.0 / np.sqrt(fan_in)
            kw, kb = jax.random.split(k)
            W = jax.random.uniform(kw, (fan_in, fan_out), jnp.float32, -bound, bound)
            b = jax.random.uniform(kb, (fan_out,), jnp.float32, -bound, bound)
            return (W, b)
        W1a, b1a = lin(ks[2], D_IN, D_HID)
        W1b, b1b = lin(ks[3], D_HID, D_HID)
        W2a, b2a = lin(ks[4], D_HID, D_HID)
        W2b, b2b = lin(ks[5], D_HID, D_OUT)
        return {'x': x, 'edge_index': edge_index, 'W1a': W1a, 'b1a': b1a, 'W1b': W1b, 'b1b': b1b, 'W2a': W2a, 'b2a': b2a, 'W2b': W2b, 'b2b': b2b}
    _L0_gnn_all = _L0_gnn_setup()
    _L0_gnn_in = {k: v for k, v in _L0_gnn_all.items() if k in ('W1a', 'b1a', 'W1b', 'b1b', 'W2a', 'b2a', 'W2b', 'b2b')}
    del _L0_gnn_all

    def _L1_gnn_setup():
        import jax, jax.numpy as jnp
        import numpy as np
        N_NODES = 50000
        N_EDGES = 9375
        IN_DIM = 128
        HIDDEN = 128

        def _gcn_layer(x, W, b, src, dst, deg_inv_sqrt, n_nodes):
            xw = x @ W
            norm = deg_inv_sqrt[src] * deg_inv_sqrt[dst]
            msg = xw[src] * norm[:, None]
            agg = jax.ops.segment_sum(msg, dst, num_segments=n_nodes)
            return agg + b
        key = jax.random.key(seed)
        k1, k2, k3, k4 = jax.random.split(key, 4)
        x = jax.random.normal(k1, (N_NODES, IN_DIM), dtype=jnp.float32)
        edge_index = jax.random.randint(k2, (2, N_EDGES), 0, N_NODES, dtype=jnp.int64)
        W1 = jax.random.normal(k3, (IN_DIM, HIDDEN), dtype=jnp.float32) / np.sqrt(IN_DIM)
        b1 = jnp.zeros((HIDDEN,), dtype=jnp.float32)
        W2 = jax.random.normal(k4, (HIDDEN, HIDDEN), dtype=jnp.float32) / np.sqrt(HIDDEN)
        b2 = jnp.zeros((HIDDEN,), dtype=jnp.float32)
        return {'x': x, 'edge_index': edge_index, 'W1': W1, 'b1': b1, 'W2': W2, 'b2': b2}
    _L1_gnn_all = _L1_gnn_setup()
    _L1_gnn_in = {k: v for k, v in _L1_gnn_all.items() if k in ('W1', 'b1', 'W2', 'b2')}
    del _L1_gnn_all
    return {'x': x, 'src': src, 'dst': dst, 'L0_gnn_W1a': _L0_gnn_in['W1a'], 'L0_gnn_b1a': _L0_gnn_in['b1a'], 'L0_gnn_W1b': _L0_gnn_in['W1b'], 'L0_gnn_b1b': _L0_gnn_in['b1b'], 'L0_gnn_W2a': _L0_gnn_in['W2a'], 'L0_gnn_b2a': _L0_gnn_in['b2a'], 'L0_gnn_W2b': _L0_gnn_in['W2b'], 'L0_gnn_b2b': _L0_gnn_in['b2b'], 'L1_gnn_W1': _L1_gnn_in['W1'], 'L1_gnn_b1': _L1_gnn_in['b1'], 'L1_gnn_W2': _L1_gnn_in['W2'], 'L1_gnn_b2': _L1_gnn_in['b2']}

def reference(x, src, dst, L0_gnn_W1a, L0_gnn_b1a, L0_gnn_W1b, L0_gnn_b1b, L0_gnn_W2a, L0_gnn_b2a, L0_gnn_W2b, L0_gnn_b2b, L1_gnn_W1, L1_gnn_b1, L1_gnn_W2, L1_gnn_b2):
    import jax
    import jax.numpy as jnp

    def _L0_gnn_ref(x, edge_index, W1a, b1a, W1b, b1b, W2a, b2a, W2b, b2b):
        import jax, jax.numpy as jnp
        import numpy as np
        N_NODES = 50000
        N_EDGES = 12500
        D_IN = 128
        D_HID = 256
        D_OUT = 128

        def _gin_conv(x, edge_index, Wa, ba, Wb, bb):
            src, dst = (edge_index[0], edge_index[1])
            agg = jax.ops.segment_sum(x[src], dst, num_segments=x.shape[0])
            h = x + agg
            h = jnp.maximum(h @ Wa + ba, 0.0)
            return h @ Wb + bb
        h = jnp.maximum(_gin_conv(x, edge_index, W1a, b1a, W1b, b1b), 0.0)
        out = _gin_conv(h, edge_index, W2a, b2a, W2b, b2b)
        return out

    def _L1_gnn_ref(x, edge_index, W1, b1, W2, b2):
        import jax, jax.numpy as jnp
        import numpy as np
        N_NODES = 50000
        N_EDGES = 9375
        IN_DIM = 128
        HIDDEN = 128

        def _gcn_layer(x, W, b, src, dst, deg_inv_sqrt, n_nodes):
            xw = x @ W
            norm = deg_inv_sqrt[src] * deg_inv_sqrt[dst]
            msg = xw[src] * norm[:, None]
            agg = jax.ops.segment_sum(msg, dst, num_segments=n_nodes)
            return agg + b
        n_nodes = x.shape[0]
        loop = jnp.arange(n_nodes, dtype=edge_index.dtype)
        src = jnp.concatenate([edge_index[0], loop])
        dst = jnp.concatenate([edge_index[1], loop])
        deg = jax.ops.segment_sum(jnp.ones_like(src, dtype=x.dtype), dst, num_segments=n_nodes)
        deg_inv_sqrt = jnp.where(deg > 0, jax.lax.rsqrt(jnp.maximum(deg, 1.0)), 0.0)
        h = jax.nn.relu(_gcn_layer(x, W1, b1, src, dst, deg_inv_sqrt, n_nodes))
        h = jax.nn.relu(_gcn_layer(h, W2, b2, src, dst, deg_inv_sqrt, n_nodes))
        return h
    edge_index = jnp.stack([src, dst])
    h = jnp.maximum(_layernorm(x, axis=-1), 0.0)
    x = x + _L0_gnn_ref(h, edge_index, L0_gnn_W1a, L0_gnn_b1a, L0_gnn_W1b, L0_gnn_b1b, L0_gnn_W2a, L0_gnn_b2a, L0_gnn_W2b, L0_gnn_b2b)
    h = jnp.maximum(_layernorm(x, axis=-1), 0.0)
    x = x + _L1_gnn_ref(h, edge_index, L1_gnn_W1, L1_gnn_b1, L1_gnn_W2, L1_gnn_b2)
    return x

_drawn_inputs = setup_inputs


def setup_inputs(seed=0):
    import zlib

    import numpy as np

    out = dict(_drawn_inputs(seed))
    spreads = {'L1_gnn_b1': (0.0, 0.1), 'L1_gnn_b2': (0.0, 0.1)}
    factors = {'L0_gnn_b1a': 8.0, 'L0_gnn_b1b': 6.437, 'L0_gnn_b2a': 4.089}
    for name, (base, spread) in spreads.items():
        noise = np.random.default_rng([zlib.crc32(name.encode()), seed]).standard_normal(out[name].shape)
        drawn = base * np.exp(spread * noise) if base else spread * noise
        out[name] = jnp.asarray(drawn.astype(out[name].dtype))
    for name, factor in factors.items():
        out[name] = (out[name] * factor).astype(out[name].dtype)
    return out
```

```python
import concourse.bass as bass
from concourse import mybir
from contextlib import ExitStack


F32, BF16, F16, I32 = mybir.dt.float32, mybir.dt.bfloat16, mybir.dt.float16, mybir.dt.int32
F32R = mybir.dt.float32r
ALU = mybir.AluOpType
ACT = mybir.ActivationFunctionType
AXX = mybir.AxisListType.X

P = 128
T = 4
R = P * T
W = 3
WP = [44, 44, 40]
W0 = [0, 44, 88]
D, DH = 128, 256
EPS = 1e-5
FAR = 1 << 20
START = 6


def ds(start, size):
    return bass.ds(start, size)


def product(nc, acc, hi, lo, moving_hi, moving_lo, start, stop):
    nc.tensor.matmul(acc, lo, moving_hi, start=start, stop=False)
    nc.tensor.matmul(acc, hi, moving_lo, start=False, stop=False)
    return nc.tensor.matmul(acc, hi, moving_hi, start=False, stop=stop)


W_AT, W_COLS = {}, 0
for _name, _k, _n in (("w1a", 1, DH), ("w1b", 2, DH), ("w2a", 2, DH), ("w2b", 2, D), ("wg1", 1, D), ("wg2", 1, D)):
    W_AT[_name] = (W_COLS, _n)
    W_COLS += _k * _n
BIAS_AT, BIAS_COLS = {}, 0
for _name, _n in (("b1b", DH), ("b2b", D), ("b1a", DH), ("b2a", DH)):
    BIAS_AT[_name] = BIAS_COLS
    BIAS_COLS += _n


def weight(c, name, k, lo=0, hi=None):
    at, n = W_AT[name]
    cols = slice(at + k * n + lo, at + k * n + (n if hi is None else hi))
    return c["w_hi"][:, cols], c["w_lo"][:, cols]


def bias_parts(c, name, lo, hi):
    return c["bias3"][:, BIAS_AT[name] + lo:BIAS_AT[name] + hi]


def f32(ap):
    return ap.bitcast(F32)


class Shapes:
    def __init__(self, n, e):
        self.N, self.E = n, e
        self.S = -(-n // R)
        self.S += self.S % 2
        self.NP = self.S * R
        self.LAST = (n - (self.S - 1) * R) // T
        assert n % T == 0 and self.LAST > 0 and self.S >= START + 12
        self.NB = -(-self.S // P)
        while self.S % self.NB:
            self.NB += 1
        self.SB = self.S // self.NB
        self.EP = max(k for k in range(1, P + 1) if e % k == 0)
        self.EC = e // self.EP
        self.ER = -(-e // P)
        assert self.EC % 4 == 0 and e % P


def hold(engine, sem, value, passed):
    engine.wait_ge(sem, value)
    if not isinstance(value, int):
        engine.sem_inc(passed, 1)


def count_of(s, p, slots=2):
    return (s - p) * (16 // slots) + 16


def run_pipeline(engine, sh, step, first, last, slots=2):
    start = -(-START // slots) * slots
    stop = start + (sh.S - 3 - slots // 2 - start) // slots * slots
    for s in range(first, start):
        step(s, s % slots)
    with engine.Fori(start, stop - slots + 1, slots) as i:
        for p in range(slots):
            step(i + p, p)
    for s in range(stop, last + 1):
        step(s, s % slots)


def node_rows(table, s, f):
    return table[ds(s * R, R), 0:f].rearrange("(p t) f -> p (t f)", t=T)


def flat(ap):
    return ap.rearrange("p t f -> p (t f)")


def windows(ap):
    return ap.rearrange("p (t q) -> p t q", t=T)


def wide(ap, n):
    return ap.unsqueeze(2).to_broadcast([ap.shape[0], ap.shape[1], n])


def graph_kernel(nc, x, src, dst, w1a, b1a, w1b, b1b, w2a, b2a, w2b, b2b, wg1, bg1, wg2, bg2, out):
    sh = Shapes(x.shape[0], src.shape[0])
    with ExitStack() as ctx:
        sb = lambda name, shape, dt=F32: ctx.enter_context(nc.sbuf_tensor(name, shape, dt))
        tables = {
            "h1": nc.dram_tensor("h1", (sh.NP, DH), F32).ap(),
            "y1": nc.dram_tensor("y1", (sh.NP, D), F32).ap(),
            "y2": nc.dram_tensor("y2", (sh.NP, D), F32).ap(),
            "x1": nc.dram_tensor("x1", (sh.NP, D), F32).ap(),
            "sum128": nc.dram_tensor("sum128", (sh.NP + P, D), F32).ap(),
            "sum256": nc.dram_tensor("sum256", (sh.NP + P, DH), F32).ap(),
            "edges": nc.dram_tensor("edges", (sh.ER + 1, 2 * P), I32).ap(),
        }
        c = {
            "ident": sb("ident", [P, P]),
            "iota": sb("iota", [P, T, WP[0]], F16),
            "eps": sb("eps", [P, 1]),
            "ones3": sb("ones3", [P, R], BF16),
            "bias3": sb("bias3", [P, BIAS_COLS], BF16),
            "w_hi": sb("w_hi", [P, W_COLS], F32R),
            "w_lo": sb("w_lo", [P, W_COLS], F32R),
            "bg1": sb("bg1_sb", [P, D]),
            "bg2": sb("bg2_sb", [P, D]),
            "idx": sb("idx", [P, sh.S * W], I32),
            "key": sb("key", [P, sh.S * W]),
            "sqdeg": sb("sqdeg", [P, sh.S * T]),
            "rsdeg": sb("rsdeg", [P, sh.S * T]),
            "rdeg": sb("rdeg", [P, sh.S * T]),
            "sp_passed": ctx.enter_context(nc.semaphore("sp_passed")),
            "pool_passed": ctx.enter_context(nc.semaphore("pool_passed")),
            "flag": sb("flag_f", [P, 2]),
            "flag_int": sb("flag_int", [P, 1], I32),
        }
        prepare(nc, sh, c, tables, src, dst, dict(w1a=w1a, w1b=w1b, w2a=w2a, w2b=w2b, wg1=wg1, wg2=wg2,
                                                  b1a=b1a, b2a=b2a, b1b=b1b, b2b=b2b, bg1=bg1, bg2=bg2))
        general_pass(nc, sh, c, tables, "g1", x, tables["sum128"], D, normed=True)
        gin_first(nc, sh, c, tables, x)
        general_pass(nc, sh, c, tables, "g2", tables["h1"], tables["sum256"], DH, normed=False)
        gin_second(nc, sh, c, tables, x)
        general_pass(nc, sh, c, tables, "g3", tables["y1"], tables["sum128"], D, normed=False)
        gcn(nc, sh, c, tables, "c1", tables["y1"], c["bg1"], out=tables["y2"], final=False)
        general_pass(nc, sh, c, tables, "g4", tables["y2"], tables["sum128"], D, normed=False)
        gcn(nc, sh, c, tables, "c2", tables["y2"], c["bg2"], out=out, final=True)


def prepare(nc, sh, c, tables, src, dst, given):
    S, SB, NB, EP, EC = sh.S, sh.SB, sh.NB, sh.EP, sh.EC
    G = NB * W
    NCOL = S * T
    edges = tables["edges"]
    full, rest = sh.E // P, sh.E % P
    SPLITS = [(a, min(a + 512, NCOL)) for a in range(0, NCOL, 512)]
    D_COUNTS = 5 + len(SPLITS) + 2
    D_DEG = D_COUNTS + 1
    D_TOT = D_DEG + 4
    D_ROWS = D_TOT + 6
    D_MATCHED = D_ROWS + 11 + 7 * (1 + G) + G + 1 + W + 1
    D_KEYS = D_MATCHED + 3
    with ExitStack() as ctx:
        sb = lambda name, shape, dt=F32: ctx.enter_context(nc.sbuf_tensor(name, shape, dt))
        ps = lambda name: ctx.enter_context(nc.psum_tensor(name, [P, 512], F32))
        sem = lambda name: ctx.enter_context(nc.semaphore(name))
        dsti = sb("dsti", [EP, EC], I32)
        part_i = sb("part_i", [EP, EC], I32)
        colh_i = sb("colh_i", [EP, EC], I32)
        coll_i = sb("coll_i", [EP, EC], I32)
        part_f = sb("part_f", [EP, EC])
        col_f = sb("col_f", [EP, EC])
        iota_p = sb("iota_p", [EP, P], F16)
        iota_c = sb("iota_c", [EP, NCOL], F16)
        hot_p = sb("hot_p", [EP, 4, P], BF16)
        hot_c = sb("hot_c", [EP, 4, NCOL], BF16)
        counts = sb("counts", [P, NCOL])
        deg = sb("deg", [P, NCOL])
        mask_v = sb("mask_v", [P, W])
        mask_lo = sb("mask_lo", [P, W])
        mask = sb("mask", [P, W])
        tri = sb("tri", [SB, SB])
        ones = sb("ones", [P, P])
        cw = sb("cw", [SB, NB, W])
        two = sb("two", [SB, NB])
        tot = sb("tot", [SB, NB])
        starts = sb("starts", [SB, NB, W])
        starts_i = sb("starts_i", [SB, G], I32)
        rows_i = sb("rows_i", [SB, 2, G], I32)
        bits_i = sb("bits_i", [SB, 7, G], I32)
        bits = sb("bits", [SB, 7, G])
        base_i = sb("base_i", [SB, NB, W], I32)
        base = sb("base", [SB, G])
        got = sb("got", [SB, G, 2, 2 * P], I32)
        runs = sb("runs", [SB, G, 2, 2 * P])
        diff = sb("diff", [SB, G, 2, 2 * P])
        runs_b = sb("runs_b", [SB, G, 2, 2 * P])
        keys = sb("keys", [SB, G, P])
        in_lo = sb("in_lo", [SB, G, P])
        in_win = sb("in_win", [SB, G, P])
        matched = sb("matched", [SB, 1])
        pad_src = sb("pad_src", [1, P], I32)
        pad_dst = sb("pad_dst", [1, P], I32)
        brow = sb("brow", [1, BIAS_COLS])
        bres = sb("bres", [1, 2, BIAS_COLS])
        bpart = sb("bpart", [1, 3, BIAS_COLS], BF16)
        w_all = sb("w_all", [P, W_COLS])
        bank = [ps(f"pb{i}") for i in range(6)]
        consts = sem("p_consts")
        edges_in, pad_in, weights_in = sem("p_edges_in"), sem("p_pad_in"), sem("p_weights_in")
        dst_in, edges_done, rows_got = sem("p_dst_in"), sem("p_edges_done"), sem("p_rows_got")
        hot_ready, counted, d, a, pe_done = sem("p_hot"), sem("p_counted"), sem("p_dve"), sem("p_act"), sem("p_pe")
        bias_row_in, bias_split, bias_in = sem("p_bias_row"), sem("p_bias_split"), sem("p_bias_in")
        w_split = sem("p_w_split")
        n_consts = [0]

        with nc.Block() as block:
            @block.gpsimd
            def _(pool):
                def made(ins):
                    n_consts[0] += 1
                    ins.then_inc(consts, 1)
                made(pool.iota(iota_p[:, :], pattern=[[1, P]], base=0, channel_multiplier=0,
                               allow_small_or_imprecise_dtypes=True))
                made(pool.iota(iota_c[:, :], pattern=[[1, NCOL]], base=0, channel_multiplier=0,
                               allow_small_or_imprecise_dtypes=True))
                made(pool.memset(pad_src[:, :], 0))
                made(pool.memset(pad_dst[:, :], FAR))
                made(pool.memset(c["ident"][:, :], 0.0))
                made(pool.memset(tri[:, :], 0.0))
                made(pool.memset(ones[:, :], 1.0))
                made(pool.memset(c["ones3"][:, :], 1.0))
                made(pool.memset(c["bias3"][:, :], 0.0))
                made(pool.memset(c["eps"][:, :], EPS))
                made(pool.iota(c["iota"][:, :, :], pattern=[[1, T], [T, WP[0]]], base=0, channel_multiplier=0,
                               allow_small_or_imprecise_dtypes=True))
                made(pool.iota(mask_v[:, :], pattern=[[-WP[0], W]], base=0, channel_multiplier=1,
                               allow_small_or_imprecise_dtypes=True))
                for b in range(NB):
                    made(pool.iota(base_i[:, b, :], pattern=[[T * WP[0], W]], base=b * SB * R,
                                   channel_multiplier=R))
                pool.wait_ge(consts, n_consts[0])
                made(pool.affine_select(out=c["ident"][:, :], in_=c["ident"][:, :], compare_op=ALU.not_equal,
                                        fill=1.0, base=0, pattern=[[-1, P]], channel_multiplier=1))
                made(pool.affine_select(out=tri[:, :], in_=tri[:, :], compare_op=ALU.is_ge,
                                        fill=1.0, base=0, pattern=[[-1, SB]], channel_multiplier=1))
                pool.wait_ge(edges_done, 16)
                pool.wait_ge(d, D_ROWS)
                for g in range(G):
                    for r in range(2):
                        pool.indirect_dma_start(got[:, g, r, :], None, edges,
                                                bass.IndirectOffsetOnAxis(ap=rows_i[:, r, g:g + 1], axis=0)
                                                ).then_inc(rows_got, 16)

            @block.sync
            def _(sp):
                sp.dma_start(dsti[:, :], dst.rearrange("(p c) -> p c", p=EP)).then_inc(dst_in, 16)
                n = 0
                for kind, given_list in enumerate((src, dst)):
                    lane = slice(kind * P, (kind + 1) * P)
                    sp.dma_start(edges[0:full, lane],
                                 given_list[0:full * P].rearrange("(r c) -> r c", c=P)).then_inc(edges_in, 16)
                    sp.dma_start(edges[full:full + 1, kind * P:kind * P + rest],
                                 given_list[full * P:sh.E].rearrange("(r c) -> r c", r=1)).then_inc(edges_in, 16)
                    n += 2
                sp.wait_ge(consts, 4)
                for kind, pad in enumerate((pad_src, pad_dst)):
                    sp.dma_start(edges[full:full + 1, kind * P + rest:(kind + 1) * P],
                                 pad[:, 0:P - rest]).then_inc(pad_in, 16)
                    sp.dma_start(edges[full + 1:full + 2, kind * P:(kind + 1) * P], pad[:, :]).then_inc(pad_in, 16)
                sp.wait_ge(edges_in, 16 * n)
                sp.wait_ge(pad_in, 64)
                sp.sem_inc(edges_done, 16)

            @block.scalar
            def _(act):
                for name, at in BIAS_AT.items():
                    act.dma_start(brow[:, at:at + given[name].shape[0]],
                                  given[name].rearrange("(r c) -> r c", r=1)).then_inc(bias_row_in, 16)
                loads = [
                    (c["bg1"][:, :], given["bg1"].partition_broadcast(P)),
                    (c["bg2"][:, :], given["bg2"].partition_broadcast(P)),
                ]
                for name, (at, n) in W_AT.items():
                    k = given[name].shape[0] // P
                    loads.append((w_all[:, at:at + k * n].rearrange("p (k n) -> p k n", k=k),
                                  given[name].rearrange("(k p) n -> p k n", p=P)))
                for to, frm in loads:
                    act.dma_start(to, frm).then_inc(weights_in, 16)
                act.wait_ge(weights_in, 16 * len(loads))
                nc.scalar.activation(c["w_hi"][:, :], w_all[:, :], ACT.Copy).then_inc(w_split, 1)
                act.wait_ge(bias_split, 5)
                act.wait_ge(consts, n_consts[0])
                act.dma_start(c["bias3"][0:3, :], bpart[0:1, :, :]).then_inc(bias_in, 16)
                act.wait_ge(d, D_DEG)
                nc.scalar.activation(c["sqdeg"][:, :], deg[:, :], ACT.Sqrt).then_inc(a, 1)
                act.wait_ge(bias_in, 16)

            @block.tensor
            def _(pe):
                def count_step(c0, u, first, last):
                    for n, (lo, hi) in enumerate(SPLITS):
                        ins = nc.tensor.matmul(bank[n][:, 0:hi - lo], hot_p[:, u, :], hot_c[:, u, lo:hi],
                                               start=first, stop=last)
                    ins.then_inc(counted, 1)
                for u in range(4):
                    pe.wait_ge(hot_ready, u + 1)
                    count_step(0, u, u == 0, False)
                with pe.Fori(4, EC - 7, 4) as i:
                    for u in range(4):
                        pe.wait_ge(hot_ready, i + (u + 1))
                        count_step(i, u, False, False)
                for u in range(4):
                    pe.wait_ge(hot_ready, EC - 4 + u + 1)
                    count_step(EC - 4, u, False, u == 3)
                pe.wait_ge(d, D_COUNTS)
                for b in range(NB):
                    for t in range(T):
                        ins = nc.tensor.matmul(bank[2][0:SB, b * W:(b + 1) * W],
                                               counts[:, b * SB * T + t:(b + 1) * SB * T:T], mask[:, :],
                                               start=t == 0, stop=t == T - 1)
                ins.then_inc(pe_done, 1)
                pe.wait_ge(d, D_TOT)
                for b in range(NB):
                    for bb in range(b + 1):
                        ins = nc.tensor.matmul(bank[3][0:SB, b:b + 1], tri[:, :] if bb == b else ones[0:SB, 0:SB],
                                               tot[:, bb:bb + 1], start=bb == 0, stop=bb == b)
                ins.then_inc(pe_done, 1)
                pe.wait_ge(d, D_MATCHED)
                nc.tensor.matmul(bank[3][:, 8:9], ones[0:SB, :], matched[:, :], start=True, stop=True).then_inc(pe_done, 1)
                for g in range(G):
                    nc.tensor.matmul(bank[4 + g // W % 2][:, (g % W) * P:(g % W) * P + SB], runs_b[:, g, 0, 0:P],
                                     c["ident"][0:SB, 0:SB], is_transpose=True, start=True, stop=True)
                    ins = nc.tensor.matmul(bank[g // W % 2][:, (g % W) * P:(g % W) * P + SB], keys[:, g, :],
                                           c["ident"][0:SB, 0:SB], is_transpose=True, start=True, stop=True)
                    if g % W == W - 1:
                        ins.then_inc(pe_done, 1)
                        if g < G - 1 and g // W >= 1:
                            pe.wait_ge(d, D_KEYS + 2 * W * (g // W))

            @block.vector
            def _(dve):
                at = [0]

                def link(ins, wait=True):
                    at[0] += 1
                    ins.then_inc(d, 1)
                    if wait:
                        dve.wait_ge(d, at[0])
                dve.wait_ge(dst_in, 16)
                link(nc.vector.tensor_scalar(part_i[:, :], dsti[:, :], 2, 127, ALU.logical_shift_right, ALU.bitwise_and), False)
                link(nc.vector.tensor_scalar(colh_i[:, :], dsti[:, :], 9, 2, ALU.logical_shift_right, ALU.logical_shift_left), False)
                link(nc.vector.tensor_scalar(coll_i[:, :], dsti[:, :], 3, None, ALU.bitwise_and))
                link(nc.vector.tensor_copy(part_f[:, :], part_i[:, :]), False)
                link(nc.vector.tensor_tensor(col_f[:, :], colh_i[:, :], coll_i[:, :], ALU.add))
                dve.wait_ge(consts, 2)

                def hot_step(i, u):
                    nc.vector.tensor_scalar(hot_p[:, u, :], iota_p[:, :], part_f[:, ds(i + u, 1)], None, ALU.is_equal)
                    nc.vector.tensor_scalar(hot_c[:, u, :], iota_c[:, :], col_f[:, ds(i + u, 1)], None,
                                            ALU.is_equal).then_inc(hot_ready, 1)
                for u in range(4):
                    hot_step(0, u)
                with dve.Fori(4, EC - 3, 4) as i:
                    for u in range(4):
                        dve.wait_ge(counted, i + (u - 3))
                        hot_step(i, u)
                dve.wait_ge(counted, EC)
                for n, (lo, hi) in enumerate(SPLITS):
                    link(nc.vector.tensor_copy(counts[:, lo:hi], bank[n][:, 0:hi - lo]), False)
                dve.wait_ge(consts, n_consts[0])
                link(nc.vector.tensor_scalar(mask_lo[:, :], mask_v[:, :], 0.0, None, ALU.is_ge))
                link(nc.vector.scalar_tensor_tensor(out=mask[:, :], in0=mask_v[:, :], scalar=float(WP[0]),
                                                    in1=mask_lo[:, :], op0=ALU.is_lt, op1=ALU.mult))
                assert at[0] == D_COUNTS
                link(nc.vector.tensor_scalar(deg[:, :], counts[:, :], 1.0, None, ALU.add))
                assert at[0] == D_DEG
                link(nc.vector.reciprocal(c["rdeg"][:, :], deg[:, :]), False)
                dve.wait_ge(pe_done, 1)
                link(nc.vector.tensor_copy(cw[:, :, :], bank[2][0:SB, 0:G].rearrange("p (b w) -> p b w", w=W)))
                link(nc.vector.tensor_tensor(two[:, :], cw[:, :, 0], cw[:, :, 1], ALU.add))
                link(nc.vector.tensor_tensor(tot[:, :], two[:, :], cw[:, :, 2], ALU.add))
                assert at[0] == D_TOT
                dve.wait_ge(pe_done, 2)
                link(nc.vector.tensor_copy(starts[:, :, 0], bank[3][0:SB, 0:NB]))
                link(nc.vector.tensor_tensor(starts[:, :, 1], starts[:, :, 0], cw[:, :, 0], ALU.add), False)
                link(nc.vector.tensor_tensor(starts[:, :, 2], starts[:, :, 0], two[:, :], ALU.add))
                link(nc.vector.tensor_copy(starts_i[:, :], starts[:, :, :].rearrange("p b w -> p (b w)")))
                link(nc.vector.tensor_scalar(rows_i[:, 0, :], starts_i[:, :], 7, None, ALU.logical_shift_right))
                link(nc.vector.tensor_scalar(rows_i[:, 1, :], rows_i[:, 0, :], 1, None, ALU.add))
                assert at[0] == D_ROWS
                for k in range(7):
                    link(nc.vector.tensor_scalar(bits_i[:, k, :], starts_i[:, :], k, 1,
                                                 ALU.logical_shift_right, ALU.bitwise_and), k == 6)
                link(nc.vector.tensor_copy(bits[:, :, :], bits_i[:, :, :]), False)
                link(nc.vector.tensor_copy(base[:, :], base_i[:, :, :].rearrange("p b w -> p (b w)")), False)
                dve.wait_ge(rows_got, 16 * 2 * G)
                for r in range(2):
                    link(nc.vector.tensor_copy(runs[:, :, :, r * P:(r + 1) * P],
                                               got[:, :, r, :].rearrange("p g (k e) -> p g k e", k=2)), r == 1)
                now, then = runs, runs_b
                for k in range(6, -1, -1):
                    step = 1 << k
                    length = P + step - 1
                    link(nc.vector.tensor_tensor(diff[:, :, :, 0:length], now[:, :, :, step:step + length],
                                                 now[:, :, :, 0:length], ALU.subtract))
                    for g in range(G):
                        link(nc.vector.scalar_tensor_tensor(out=then[:, g, :, 0:length], in0=diff[:, g, :, 0:length],
                                                            scalar=bits[:, k, g:g + 1], in1=now[:, g, :, 0:length],
                                                            op0=ALU.mult, op1=ALU.add), g == G - 1)
                    now, then = then, now
                assert now is runs_b
                for g in range(G):
                    link(nc.vector.tensor_scalar(keys[:, g, :], now[:, g, 1, 0:P], base[:, g:g + 1], None,
                                                 ALU.subtract), g == G - 1)
                link(nc.vector.tensor_scalar(in_lo[:, :, :], keys[:, :, :], 0.0, None, ALU.is_ge))
                for w in range(W):
                    link(nc.vector.scalar_tensor_tensor(out=in_win[:, w::W, :], in0=keys[:, w::W, :],
                                                        scalar=float(T * WP[w]), in1=in_lo[:, w::W, :],
                                                        op0=ALU.is_lt, op1=ALU.mult), w == W - 1)
                link(nc.vector.reduce_sum(matched[:, :], in_win[:, :, :].rearrange("p g e -> p (g e)"), axis=AXX))
                assert at[0] == D_MATCHED
                dve.wait_ge(pe_done, 3)
                link(nc.vector.tensor_scalar(c["flag"][:, 0:1], bank[3][:, 8:9], float(sh.E), None, ALU.is_equal), False)
                link(nc.vector.tensor_scalar(c["flag"][:, 1:2], bank[3][:, 8:9], float(sh.E), None, ALU.not_equal))
                link(nc.vector.tensor_copy(c["flag_int"][:, :], c["flag"][:, 1:2]), False)
                assert at[0] == D_KEYS
                for b in range(NB):
                    dve.wait_ge(pe_done, 4 + b)
                    for w in range(W):
                        cols = slice(b * SB * W + w, (b + 1) * SB * W, W)
                        link(nc.vector.tensor_copy(c["idx"][:, cols], bank[4 + b % 2][:, w * P:w * P + SB]), False)
                        link(nc.vector.tensor_scalar(c["key"][:, cols], bank[b % 2][:, w * P:w * P + SB],
                                                     c["flag"][:, 0:1], None, ALU.mult), False)
                dve.wait_ge(d, at[0])
                link(nc.vector.tensor_scalar(c["key"][:, :], c["key"][:, :], c["flag"][:, 1:2], None, ALU.subtract), False)
                dve.wait_ge(bias_row_in, 16 * len(BIAS_AT))
                nc.vector.tensor_copy(bpart[:, 0, :], brow[:, :]).then_inc(bias_split, 1)
                dve.wait_ge(bias_split, 1)
                nc.vector.tensor_tensor(bres[:, 0, :], brow[:, :], bpart[:, 0, :], ALU.subtract).then_inc(bias_split, 1)
                dve.wait_ge(bias_split, 2)
                nc.vector.tensor_copy(bpart[:, 1, :], bres[:, 0, :]).then_inc(bias_split, 1)
                dve.wait_ge(bias_split, 3)
                nc.vector.tensor_tensor(bres[:, 1, :], bres[:, 0, :], bpart[:, 1, :], ALU.subtract).then_inc(bias_split, 1)
                dve.wait_ge(bias_split, 4)
                nc.vector.tensor_copy(bpart[:, 2, :], bres[:, 1, :]).then_inc(bias_split, 1)
                dve.wait_ge(w_split, 1)
                nc.vector.tensor_tensor(c["w_lo"][:, :], w_all[:, :], f32(c["w_hi"][:, :]), ALU.subtract).then_inc(w_split, 1)
                dve.wait_ge(a, 1)
                link(nc.vector.reciprocal(c["rsdeg"][:, :], c["sqdeg"][:, :]))


def general_pass(nc, sh, c, tables, tag, rows, total, F, normed):
    edges = tables["edges"]
    ER = sh.ER
    with ExitStack() as ctx:
        sb = lambda name, shape, dt=F32: ctx.enter_context(nc.sbuf_tensor(f"{tag}_{name}", shape, dt))
        sem = lambda name: ctx.enter_context(nc.semaphore(f"{tag}_{name}"))
        part = sb("part", [P, T, F])
        parted = sb("parted", [P, T, F])
        st = sb("st", [P, T, 6])
        small = sb("small", [P, 8, T])
        src_i = sb("src_i", [P, 1], I32)
        dst_i = sb("dst_i", [P, 1], I32)
        to_i = sb("to_i", [P, 1], I32)
        row_i = sb("row_i", [P, P], I32)
        dst_f = sb("dst_f", [P, 1])
        row_f = sb("row_f", [P, P])
        same = sb("same", [P, P])
        before = sb("before", [P, P])
        below = sb("below", [P, P])
        spare = sb("spare", [P, 1])
        vec = sb("vec", [P, 6])
        got = sb("got", [P, F])
        msg = sb("msg", [P, F])
        old = sb("old", [P, F])
        new = sb("new", [P, F])
        zero = sb("zero", [P, F])
        sums = ctx.enter_context(nc.psum_tensor(f"{tag}_sums", [P, F], F32))
        made, copied_in, copied_out = sem("made"), sem("copied_in"), sem("copied_out")
        listed, gathered, fetched, placed = sem("listed"), sem("gathered"), sem("fetched"), sem("placed")
        d, a, summed = sem("dve"), sem("act"), sem("summed")
        K = 6 if normed else 0
        KC = 16
        with nc.Block() as block:
            def stats(dve, wait, rows_in, tiles, base, sqrt_at):
                n = tiles
                for t in range(n):
                    nc.vector.bn_stats(st[:, t, :], rows_in(t)).then_inc(d, 1)
                wait(n)
                nc.vector.tensor_tensor(small[:, 0, 0:n], st[:, 0:n, 1], st[:, 0:n, 4], ALU.add).then_inc(d, 1)
                nc.vector.tensor_tensor(small[:, 1, 0:n], st[:, 0:n, 1], st[:, 0:n, 4], ALU.subtract).then_inc(d, 1)
                nc.vector.tensor_tensor(small[:, 2, 0:n], st[:, 0:n, 2], st[:, 0:n, 5], ALU.add).then_inc(d, 1)
                wait(n + 3)
                nc.vector.scalar_tensor_tensor(out=small[:, 3, 0:n], in0=small[:, 1, 0:n], scalar=0.25,
                                               in1=small[:, 1, 0:n], op0=ALU.mult, op1=ALU.mult).then_inc(d, 1)
                wait(n + 4)
                nc.vector.scalar_tensor_tensor(out=small[:, 4, 0:n], in0=small[:, 2, 0:n], scalar=1.0 / D,
                                               in1=small[:, 3, 0:n], op0=ALU.mult, op1=ALU.add).then_inc(d, 1)
                dve.wait_ge(a, sqrt_at)
                nc.vector.reciprocal(small[:, 5, 0:n], small[:, 7, 0:n]).then_inc(d, 1)
                wait(n + 6)
                nc.vector.tensor_scalar(small[:, 6, 0:n], small[:, 0, 0:n], 0.5, None, ALU.mult).then_inc(d, 1)
                wait(n + 7)

            NS = T + 7 + T + 1
            NE = (1 + 7 + 2 if normed else 0) + 10
            BASE = sh.S * NS if normed else 0

            @block.gpsimd
            def _(pool):
                flag = pool.value_load(c["flag_int"][0:1, 0:1], min_val=0, max_val=1)
                with pool.If(flag > 0):
                    pool.memset(below[:, :], 0.0).then_inc(made, 1)
                    pool.wait_ge(made, 1)
                    pool.affine_select(out=below[:, :], in_=below[:, :], compare_op=ALU.is_ge, fill=1.0, base=0,
                                       pattern=[[1, P]], channel_multiplier=-1).then_inc(made, 1)
                    pool.memset(zero[:, :], 0.0).then_inc(made, 1)
                    pool.iota(spare[:, :], pattern=[[0, 1]], base=sh.NP, channel_multiplier=1,
                              allow_small_or_imprecise_dtypes=True).then_inc(made, 1)
                    with pool.Fori(0, ER) as i:
                        hold(pool, listed, i * 48 + 48, c["pool_passed"])
                        pool.indirect_dma_start(got[:, :], None, rows,
                                                bass.IndirectOffsetOnAxis(ap=src_i[:, :], axis=0)).then_inc(gathered, 16)
                        hold(pool, d, i * NE + (BASE + NE - 1), c["pool_passed"])
                        pool.indirect_dma_start(old[:, :], None, total,
                                                bass.IndirectOffsetOnAxis(ap=to_i[:, :], axis=0)).then_inc(fetched, 16)
                        hold(pool, d, i * NE + (BASE + NE), c["pool_passed"])
                        pool.indirect_dma_start(total, bass.IndirectOffsetOnAxis(ap=to_i[:, :], axis=0),
                                                new[:, :], None).then_inc(placed, 16)
                        hold(pool, placed, i * 16 + 16, c["pool_passed"])
                with pool.Else():
                    pool.nop()
                pool.nop()

            @block.sync
            def _(sp):
                flag = sp.value_load(c["flag_int"][0:1, 0:1], min_val=0, max_val=1)
                with sp.If(flag > 0):
                    sp.wait_ge(made, 3)
                    sp.dma_start(total[sh.NP:sh.NP + P, :], zero[:, :]).then_inc(copied_out, 16)
                    sp.wait_ge(copied_out, 16)

                    def rows_step(i, frm, to):
                        sp.dma_start(to, frm).then_inc(copied_in, 16)
                        if normed:
                            hold(sp, d, i * NS + NS, c["sp_passed"])
                            sp.dma_start(node_rows(total, i, F), flat(parted[:, :, :])).then_inc(copied_out, 16)
                        else:
                            hold(sp, copied_in, i * 16 + 16, c["sp_passed"])
                            sp.dma_start(node_rows(total, i, F), flat(part[:, :, :])).then_inc(copied_out, 16)
                        hold(sp, copied_out, i * 16 + 32, c["sp_passed"])
                    with sp.Fori(0, sh.S - 1) as i:
                        rows_step(i, node_rows(rows, i, F), flat(part[:, :, :]))
                    if normed:
                        rows_step(sh.S - 1, rows[(sh.S - 1) * R:sh.N, :].rearrange("(p t) f -> p (t f)", t=T),
                                  flat(part[0:sh.LAST, :, :]))
                    else:
                        rows_step(sh.S - 1, node_rows(rows, sh.S - 1, F), flat(part[:, :, :]))
                    with sp.Fori(0, ER) as i:
                        with nc.allow_non_contiguous_dma(reason="one edge on a partition"):
                            sp.dma_start(src_i[:, :], edges[ds(i, 1), 0:P].rearrange("r e -> e r")).then_inc(listed, 16)
                            sp.dma_start(dst_i[:, :], edges[ds(i, 1), P:2 * P].rearrange("r e -> e r")).then_inc(listed, 16)
                        sp.dma_start(row_i[:, :], edges[ds(i, 1), P:2 * P].to_broadcast([P, P])).then_inc(listed, 16)
                        hold(sp, placed, i * 16 + 16, c["sp_passed"])
                with sp.Else():
                    sp.nop()
                sp.nop()

            @block.scalar
            def _(act):
                flag = act.value_load(c["flag_int"][0:1, 0:1], min_val=0, max_val=1)
                with act.If(flag > 0):
                    if normed:
                        with act.Fori(0, sh.S) as i:
                            act.wait_ge(d, i * NS + (T + 5))
                            nc.scalar.activation(small[:, 7, 0:T], small[:, 4, 0:T], ACT.Sqrt, bias=c["eps"][:, :]).then_inc(a, 1)
                            act.wait_ge(a, i + 1)
                        with act.Fori(0, ER) as i:
                            act.wait_ge(d, i * NE + (BASE + 6))
                            nc.scalar.activation(small[:, 7, 0:1], small[:, 4, 0:1], ACT.Sqrt, bias=c["eps"][:, :]).then_inc(a, 1)
                            act.wait_ge(a, i + (sh.S + 1))
                    else:
                        act.nop()
                with act.Else():
                    act.nop()
                act.nop()

            @block.tensor
            def _(pe):
                flag = pe.value_load(c["flag_int"][0:1, 0:1], min_val=0, max_val=1)
                with pe.If(flag > 0):
                    with pe.Fori(0, ER) as i:
                        pe.wait_ge(d, i * NE + (BASE + NE - 1))
                        if not normed:
                            pe.wait_ge(gathered, i * 16 + 16)
                        nc.tensor.matmul(sums[:, :], same[:, :], (msg if normed else got)[:, :],
                                         start=True, stop=True).then_inc(summed, 1)
                with pe.Else():
                    pe.nop()
                pe.nop()

            @block.vector
            def _(dve):
                flag = dve.value_load(c["flag_int"][0:1, 0:1], min_val=0, max_val=1)
                with dve.If(flag > 0):
                    if normed:
                        with dve.Fori(0, sh.S) as i:
                            dve.wait_ge(copied_in, i * 16 + 16)
                            wait = lambda k: dve.wait_ge(d, i * NS + k)
                            stats(dve, wait, lambda t: part[:, t, :], T, 0, i + 1)
                            for t in range(T):
                                nc.vector.tensor_scalar(part[:, t, :], part[:, t, :], small[:, 6, t:t + 1],
                                                        small[:, 5, t:t + 1], ALU.subtract, ALU.mult).then_inc(d, 1)
                            wait(T + 7 + T)
                            dve.wait_ge(copied_out, i * 16 + 16)
                            nc.vector.tensor_scalar(parted[:, :, :], part[:, :, :], 0.0, None, ALU.max).then_inc(d, 1)
                            wait(NS)
                    dve.wait_ge(made, 4)
                    with dve.Fori(0, ER) as i:
                        wait = lambda k: dve.wait_ge(d, i * NE + (BASE + k))
                        k0 = 0
                        if normed:
                            dve.wait_ge(gathered, i * 16 + 16)
                            stats(dve, wait, lambda t: got[:, :], 1, 0, i + (sh.S + 1))
                            nc.vector.tensor_scalar(got[:, :], got[:, :], small[:, 6, 0:1],
                                                    small[:, 5, 0:1], ALU.subtract, ALU.mult).then_inc(d, 1)
                            wait(9)
                            nc.vector.tensor_scalar(msg[:, :], got[:, :], 0.0, None, ALU.max).then_inc(d, 1)
                            k0 = 10
                        dve.wait_ge(listed, i * 48 + 48)
                        nc.vector.tensor_copy(dst_f[:, :], dst_i[:, :]).then_inc(d, 1)
                        nc.vector.tensor_copy(row_f[:, :], row_i[:, :]).then_inc(d, 1)
                        wait(k0 + 2)
                        nc.vector.tensor_scalar(same[:, :], row_f[:, :], dst_f[:, 0:1], None, ALU.is_equal).then_inc(d, 1)
                        nc.vector.tensor_tensor(vec[:, 3:4], dst_f[:, :], spare[:, :], ALU.subtract).then_inc(d, 1)
                        wait(k0 + 4)
                        nc.vector.tensor_tensor(before[:, :], same[:, :], below[:, :], ALU.mult).then_inc(d, 1)
                        wait(k0 + 5)
                        nc.vector.reduce_sum(vec[:, 0:1], before[:, :], axis=AXX).then_inc(d, 1)
                        wait(k0 + 6)
                        nc.vector.tensor_scalar(vec[:, 1:2], vec[:, 0:1], 0.0, vec[:, 3:4], ALU.is_equal, ALU.mult).then_inc(d, 1)
                        nc.vector.tensor_scalar(vec[:, 2:3], dst_f[:, :], float(FAR), None, ALU.is_lt).then_inc(d, 1)
                        wait(k0 + 8)
                        nc.vector.scalar_tensor_tensor(out=to_i[:, :], in0=vec[:, 1:2], scalar=vec[:, 2:3],
                                                       in1=spare[:, :], op0=ALU.mult, op1=ALU.add).then_inc(d, 1)
                        dve.wait_ge(fetched, i * 16 + 16)
                        dve.wait_ge(summed, i + 1)
                        nc.vector.tensor_tensor(new[:, :], sums[:, :], old[:, :], ALU.add).then_inc(d, 1)
                        wait(k0 + 10)
                        dve.wait_ge(placed, i * 16 + 16)
                with dve.Else():
                    dve.nop()
                dve.nop()


def load_own(sp, sh, c, plain, total, body):
    flag = sp.value_load(c["flag_int"][0:1, 0:1], min_val=0, max_val=1)
    with sp.If(flag > 0):
        body(total)
        sp.nop()
    with sp.Else():
        body(plain)
        sp.nop()
    sp.nop()




def gin_first(nc, sh, c, tables, x):
    S = sh.S
    live = lambda s: not isinstance(s, int) or 0 <= s < S
    h1 = tables["h1"]
    with ExitStack() as ctx:
        sb = lambda name, shape, dt=F32: ctx.enter_context(nc.sbuf_tensor(f"a_{name}", shape, dt))
        ps = lambda name: ctx.enter_context(nc.psum_tensor(f"a_{name}", [P, 512], F32))
        sem = lambda name: ctx.enter_context(nc.semaphore(f"a_{name}"))
        TW = T + W
        xg = sb("xg", [P, 2, TW, D])
        ix = sb("ix", [P, 2, W], I32)
        st = sb("st", [P, 2, TW, 6])
        msum, mdif, vsum, msq, var, dev, rstd, mean, nmr = (
            sb(n, [P, 2, TW]) for n in ("msum", "mdif", "vsum", "msq", "var", "dev", "rstd", "mean", "nmr"))
        xn = sb("xn", [P, 2, T, D])
        gc = sb("gc", [P, 2, W, D])
        hot = sb("hot", [P, 2, W, T, WP[0]])
        ht_hi, ht_lo = sb("ht_hi", [P, 2, R], F32R), sb("ht_lo", [P, 2, R], F32R)
        at_hi, at_lo = sb("at_hi", [P, 2, 2, R], F32R), sb("at_lo", [P, 2, 2, R], F32R)
        hout = sb("hout", [P, 2, T, DH])
        psT = [ps("psT0"), ps("psT1")]
        psA = [ps("psA0"), ps("psA1")]
        psB = [ps(f"psB{i}") for i in range(2)]
        own_loaded = [sem("own_loaded0"), sem("own_loaded1")]
        gath_loaded = [sem("gath_loaded0"), sem("gath_loaded1")]
        stored = [sem("stored0"), sem("stored1")]
        ix_ready, var_ready, dev_ready, rstd_ready = sem("ix_ready"), sem("var_ready"), sem("dev_ready"), sem("rstd_ready")
        own_normed, gath_ready, small_done = sem("own_normed"), sem("gath_ready"), sem("small_done")
        t_done, t_hi, t_lo, a_done, a_hi, a_lo = (sem("t_done"), sem("t_hi"), sem("t_lo"), sem("a_done"), sem("a_hi"),
                                                  sem("a_lo"))
        b_done, b_read = sem("b_done"), sem("b_read")

        with nc.Block() as block:
            @block.sync
            def _(sp):
                def body(table):
                    def step(s, p):
                        q = 1 - p
                        if live(s + 3):
                            if live(s + 1):
                                hold(sp, own_normed, s + 2, c["sp_passed"])
                                hold(sp, gath_ready, s + 2, c["sp_passed"])
                            if isinstance(s, int) and s + 3 == S - 1:
                                rows = table[(S - 1) * R:sh.N, :].rearrange("(p t) f -> p (t f)", t=T)
                                to = flat(xg[0:sh.LAST, q, 0:T, :])
                            else:
                                rows, to = node_rows(table, s + 3, D), flat(xg[:, q, 0:T, :])
                            sp.dma_start(to, rows).then_inc(own_loaded[q], 16)
                        if live(s - 1):
                            hold(sp, b_read, s * 2, c["sp_passed"])
                            sp.dma_start(node_rows(h1, s - 1, DH), flat(hout[:, q, :, :])).then_inc(stored[q], 16)
                    run_pipeline(sp, sh, step, -3, S)
                load_own(sp, sh, c, x, tables["sum128"], body)
                sp.wait_ge(stored[0], 8 * S)
                sp.wait_ge(stored[1], 8 * S)

            @block.gpsimd
            def _(pool):
                def step(s, p):
                    q = 1 - p
                    if live(s + 3):
                        if live(s + 1):
                            hold(pool, gath_ready, s + 2, c["pool_passed"])
                        pool.tensor_copy(ix[:, q, :], c["idx"][:, ds((s + 3) * W, W)]).then_inc(ix_ready, 1)
                        hold(pool, ix_ready, s + 4, c["pool_passed"])
                        for w in range(W):
                            pool.indirect_dma_start(xg[:, q, T + w, :], None, x,
                                                    bass.IndirectOffsetOnAxis(ap=ix[:, q, w:w + 1], axis=0)
                                                    ).then_inc(gath_loaded[q], 16)
                run_pipeline(pool, sh, step, -3, S)

            @block.vector
            def _(dve):
                def step(s, p):
                    q = 1 - p
                    if live(s + 2):
                        n = s + 2
                        dve.wait_ge(own_loaded[p], count_of(n, p))
                        dve.wait_ge(gath_loaded[p], count_of(n, p) * W)
                        for t in range(TW):
                            nc.vector.bn_stats(st[:, p, t, :], xg[:, p, t, :]).then_inc(small_done, 1)
                        dve.wait_ge(small_done, n * 15 + 7)
                        nc.vector.tensor_tensor(msum[:, p, :], st[:, p, :, 1], st[:, p, :, 4], ALU.add).then_inc(small_done, 1)
                        nc.vector.tensor_tensor(mdif[:, p, :], st[:, p, :, 1], st[:, p, :, 4], ALU.subtract).then_inc(small_done, 1)
                        nc.vector.tensor_tensor(vsum[:, p, :], st[:, p, :, 2], st[:, p, :, 5], ALU.add).then_inc(small_done, 1)
                        dve.wait_ge(small_done, n * 15 + 9)
                        nc.vector.scalar_tensor_tensor(out=msq[:, p, :], in0=mdif[:, p, :], scalar=0.25, in1=mdif[:, p, :],
                                                       op0=ALU.mult, op1=ALU.mult).then_inc(small_done, 1)
                        dve.wait_ge(small_done, n * 15 + 11)
                        nc.vector.scalar_tensor_tensor(out=var[:, p, :], in0=vsum[:, p, :], scalar=1.0 / D, in1=msq[:, p, :],
                                                       op0=ALU.mult, op1=ALU.add).then_inc(var_ready, 1)
                        nc.vector.tensor_scalar(mean[:, p, :], msum[:, p, :], 0.5, None, ALU.mult).then_inc(small_done, 1)
                    if live(s):
                        for m in range(2):
                            dve.wait_ge(a_hi, s * 2 + (m + 1))
                            nc.vector.scalar_tensor_tensor(out=at_lo[:, p, m, :], in0=psA[m][:, :], scalar=0.0,
                                                           in1=f32(at_hi[:, p, m, :]), op0=ALU.max,
                                                           op1=ALU.subtract).then_inc(a_lo, 1)
                    if live(s + 1):
                        dve.wait_ge(t_hi, s + 2)
                        nc.vector.tensor_tensor(ht_lo[:, q, :], psT[q][:, :], f32(ht_hi[:, q, :]), ALU.subtract).then_inc(t_lo, 1)
                    if live(s + 2):
                        n = s + 2
                        dve.wait_ge(dev_ready, n + 1)
                        nc.vector.reciprocal(rstd[:, p, :], dev[:, p, :]).then_inc(small_done, 1)
                        dve.wait_ge(small_done, n * 15 + 13)
                        nc.vector.scalar_tensor_tensor(out=nmr[:, p, 0:T], in0=mean[:, p, 0:T], scalar=-1.0, in1=rstd[:, p, 0:T],
                                                       op0=ALU.mult, op1=ALU.mult).then_inc(small_done, 1)
                        dve.wait_ge(small_done, n * 15 + 14)
                        nc.vector.tensor_scalar(nmr[:, p, 0:T], nmr[:, p, 0:T], c["flag"][:, 0:1], None,
                                                ALU.mult).then_inc(rstd_ready, 1)
                        nc.vector.tensor_scalar(rstd[:, p, 0:T], rstd[:, p, 0:T], c["flag"][:, 0:1], c["flag"][:, 1:2],
                                                ALU.mult, ALU.add).then_inc(rstd_ready, 1)
                        if live(n - 2):
                            dve.wait_ge(t_done, s + 1)
                        for w in range(W):
                            nc.vector.tensor_scalar(gc[:, p, w, :], xg[:, p, T + w, :], mean[:, p, T + w:T + w + 1], 0.0,
                                                    ALU.subtract, ALU.max)
                        for w in range(W):
                            ins = nc.vector.tensor_scalar(hot[:, p, w, :, 0:WP[w]], c["iota"][:, :, 0:WP[w]],
                                                          c["key"][:, ds(n * W + w, 1)], rstd[:, p, T + w:T + w + 1],
                                                          ALU.is_equal, ALU.mult)
                        ins.then_inc(gath_ready, 1)
                        nc.vector.tensor_scalar(msq[:, p, :], mean[:, p, :], 1.0, None, ALU.mult).then_inc(small_done, 1)
                run_pipeline(dve, sh, step, -2, S)

            @block.scalar
            def _(act):
                def step(s, p):
                    q = 1 - p
                    if live(s):
                        for m in range(2):
                            act.wait_ge(a_done, s * 2 + (m + 1))
                            if live(s - 2) and m == 0:
                                act.wait_ge(b_done, (s - 1) * 2)
                            nc.scalar.activation(at_hi[:, p, m, :], psA[m][:, :], ACT.Relu).then_inc(a_hi, 1)
                    if live(s + 2):
                        act.wait_ge(var_ready, s + 3)
                        nc.scalar.activation(dev[:, p, :], var[:, p, :], ACT.Sqrt, bias=c["eps"][:, :]).then_inc(dev_ready, 1)
                    if live(s + 1):
                        act.wait_ge(t_done, s + 2)
                        nc.scalar.activation(ht_hi[:, q, :], psT[q][:, :], ACT.Copy).then_inc(t_hi, 1)
                    if live(s + 2):
                        act.wait_ge(rstd_ready, (s + 3) * 2)
                        if live(s):
                            act.wait_ge(t_done, s + 1)
                        for t in range(T):
                            ins = nc.scalar.activation(xn[:, p, t, :], xg[:, p, t, :], ACT.Relu,
                                                       bias=nmr[:, p, t:t + 1], scale=rstd[:, p, t:t + 1])
                        ins.then_inc(own_normed, 1)
                    if live(s - 1):
                        if live(s - 3):
                            act.wait_ge(stored[q], count_of(s - 3, q))
                        for half in range(2):
                            act.wait_ge(b_done, s * 2 - (1 - half))
                            nc.scalar.activation(flat(hout[:, q, 2 * half:2 * half + 2, :]), psB[half][:, :],
                                                 ACT.Relu).then_inc(b_read, 1)
                run_pipeline(act, sh, step, -2, S)

            @block.tensor
            def _(pe):
                def step(s, p):
                    q = 1 - p
                    if live(s):
                        pe.wait_ge(t_lo, s + 1)
                        if live(s - 1):
                            pe.wait_ge(a_lo, s * 2)
                        for m in range(2):
                            nc.tensor.matmul(psA[m][:, :], bias_parts(c, "b1a", m * P, (m + 1) * P), c["ones3"][:, :],
                                             start=True, stop=False)
                            product(nc, psA[m][:, :], *weight(c, "w1a", 0, m * P, (m + 1) * P), ht_hi[:, p, :],
                                    ht_lo[:, p, :], False, True).then_inc(a_done, 1)
                    if live(s + 1):
                        pe.wait_ge(own_normed, s + 2)
                        pe.wait_ge(gath_ready, s + 2)
                        if live(s - 1):
                            pe.wait_ge(t_lo, s)
                        for t in range(T):
                            nc.tensor.matmul(psT[q][:, t * P:(t + 1) * P], xn[:, q, t, :], c["ident"][:, :],
                                             is_transpose=True, start=t == 0, stop=False)
                        for w in range(W):
                            ins = nc.tensor.matmul(windows(psT[q][:, :])[:, :, W0[w]:W0[w] + WP[w]], gc[:, q, w, :],
                                                   hot[:, q, w, :, 0:WP[w]], start=False, stop=w == W - 1)
                        ins.then_inc(t_done, 1)
                    if live(s - 1):
                        pe.wait_ge(a_lo, s * 2)
                        if live(s - 2):
                            pe.wait_ge(b_read, (s - 1) * 2)
                        for t in range(T):
                            acc = psB[t // 2][:, (t % 2) * DH:(t % 2 + 1) * DH]
                            nc.tensor.matmul(acc, c["ones3"][:, 0:P], bias_parts(c, "b1b", 0, DH), start=t % 2 == 0, stop=False)
                            for k in range(2):
                                rows = at_hi[:, q, k, t * P:(t + 1) * P], at_lo[:, q, k, t * P:(t + 1) * P]
                                ins = product(nc, acc, *rows, *weight(c, "w1b", k), False, t % 2 == 1 and k == 1)
                            if t % 2 == 1:
                                ins.then_inc(b_done, 1)
                run_pipeline(pe, sh, step, -1, S)


def gin_second(nc, sh, c, tables, x):
    S = sh.S
    live = lambda s: not isinstance(s, int) or 0 <= s < S
    h1, x1, y1 = tables["h1"], tables["x1"], tables["y1"]
    with ExitStack() as ctx:
        sb = lambda name, shape, dt=F32: ctx.enter_context(nc.sbuf_tensor(f"b_{name}", shape, dt))
        ps = lambda name: ctx.enter_context(nc.psum_tensor(f"b_{name}", [P, 512], F32))
        sem = lambda name: ctx.enter_context(nc.semaphore(f"b_{name}"))
        own = sb("own", [P, 2, T, DH])
        gat = sb("gat", [P, 2, W, DH])
        gat_hi, gat_lo = sb("gat_hi", [P, 2, W, DH], F32R), sb("gat_lo", [P, 2, W, DH], F32R)
        ix = sb("ix", [P, 2, W], I32)
        hot = sb("hot", [P, 2, W, T, WP[0]], F32R)
        ht_hi, ht_lo = sb("ht_hi", [P, 2, 2, R], F32R), sb("ht_lo", [P, 2, 2, R], F32R)
        at_hi, at_lo = sb("at_hi", [P, 2, 2, R], F32R), sb("at_lo", [P, 2, 2, R], F32R)
        xr = sb("xr", [P, 2, T, D])
        xs = sb("xs", [P, 2, T, D])
        hn = sb("hn", [P, 2, T, D])
        hnt_hi, hnt_lo = sb("hnt_hi", [P, 2, R], F32R), sb("hnt_lo", [P, 2, R], F32R)
        yo = sb("yo", [P, 2, T, D])
        st = sb("st", [P, 2, T, 6])
        msum, mdif, vsum, msq, var, dev, rstd, nmr = (
            sb(n, [P, 2, T]) for n in ("msum", "mdif", "vsum", "msq", "var", "dev", "rstd", "nmr"))
        psT = [ps("psT0"), ps("psT1")]
        psA = [ps("psA0"), ps("psA1")]
        psB, psH, psY = ps("psB"), ps("psH"), ps("psY")
        own_loaded = [sem("own_loaded0"), sem("own_loaded1")]
        gath_loaded = [sem("gath_loaded0"), sem("gath_loaded1")]
        x_loaded = [sem("x_loaded0"), sem("x_loaded1")]
        x_stored = [sem("x_stored0"), sem("x_stored1")]
        y_stored = [sem("y_stored0"), sem("y_stored1")]
        ix_ready, hot_ready, small_done = sem("ix_ready"), sem("hot_ready"), sem("small_done")
        x_ready, var_ready, dev_ready, rstd_ready, normed = (sem("x_ready"), sem("var_ready"), sem("dev_ready"),
                                                             sem("rstd_ready"), sem("normed"))
        t_done, t_hi, t_lo, a_done, a_hi, a_lo = (sem("t_done"), sem("t_hi"), sem("t_lo"), sem("a_done"), sem("a_hi"),
                                                  sem("a_lo"))
        b_done, h_done, h_hi, h_lo, y_done, y_read = (sem("b_done"), sem("h_done"), sem("h_hi"), sem("h_lo"),
                                                      sem("y_done"), sem("y_read"))
        gath_hi, gath_lo = sem("gath_hi"), sem("gath_lo")

        with nc.Block() as block:
            @block.sync
            def _(sp):
                def body(table):
                    def step(s, p):
                        q = 1 - p
                        if live(s + 3):
                            if live(s + 1):
                                hold(sp, t_done, (s + 2) * 2, c["sp_passed"])
                            sp.dma_start(flat(own[:, q, :, :]), node_rows(table, s + 3, DH)).then_inc(own_loaded[q], 16)
                        if live(s):
                            if live(s - 2):
                                hold(sp, x_ready, s - 1, c["sp_passed"])
                            if isinstance(s, int) and s == S - 1:
                                rows = x[(S - 1) * R:sh.N, :].rearrange("(p t) f -> p (t f)", t=T)
                                to = flat(xr[0:sh.LAST, p, :, :])
                            else:
                                rows, to = node_rows(x, s, D), flat(xr[:, p, :, :])
                            sp.dma_start(to, rows).then_inc(x_loaded[p], 16)
                        if live(s - 2):
                            hold(sp, x_ready, s - 1, c["sp_passed"])
                            sp.dma_start(node_rows(x1, s - 2, D), flat(xs[:, p, :, :])).then_inc(x_stored[p], 16)
                        if live(s - 4):
                            hold(sp, y_read, s - 3, c["sp_passed"])
                            sp.dma_start(node_rows(y1, s - 4, D), flat(yo[:, p, :, :])).then_inc(y_stored[p], 16)
                    run_pipeline(sp, sh, step, -3, S + 3)
                load_own(sp, sh, c, h1, tables["sum256"], body)
                for done in x_stored + y_stored:
                    sp.wait_ge(done, 8 * S)

            @block.gpsimd
            def _(pool):
                def step(s, p):
                    q = 1 - p
                    if live(s + 3):
                        if live(s + 1):
                            hold(pool, gath_lo, s + 2, c["pool_passed"])
                        pool.tensor_copy(ix[:, q, :], c["idx"][:, ds((s + 3) * W, W)]).then_inc(ix_ready, 1)
                        hold(pool, ix_ready, s + 4, c["pool_passed"])
                        for w in range(W):
                            pool.indirect_dma_start(gat[:, q, w, :], None, h1,
                                                    bass.IndirectOffsetOnAxis(ap=ix[:, q, w:w + 1], axis=0)
                                                    ).then_inc(gath_loaded[q], 16)
                    if live(s + 2):
                        hold(pool, gath_hi, s + 3, c["pool_passed"])
                        if live(s):
                            hold(pool, t_done, (s + 1) * 2, c["pool_passed"])
                        pool.tensor_tensor(gat_lo[:, p, :, :], gat[:, p, :, :], f32(gat_hi[:, p, :, :]),
                                           ALU.subtract).then_inc(gath_lo, 1)
                run_pipeline(pool, sh, step, -3, S)

            @block.vector
            def _(dve):
                def step(s, p):
                    q = 1 - p
                    if live(s - 2):
                        n = s - 2
                        for t in range(T):
                            nc.vector.bn_stats(st[:, p, t, :], xs[:, p, t, :]).then_inc(small_done, 1)
                        dve.wait_ge(small_done, n * 9 + 4)
                        nc.vector.tensor_tensor(mdif[:, p, :], st[:, p, :, 1], st[:, p, :, 4], ALU.subtract).then_inc(small_done, 1)
                        nc.vector.tensor_tensor(vsum[:, p, :], st[:, p, :, 2], st[:, p, :, 5], ALU.add).then_inc(small_done, 1)
                        nc.vector.tensor_tensor(msum[:, p, :], st[:, p, :, 1], st[:, p, :, 4], ALU.add).then_inc(small_done, 1)
                        dve.wait_ge(small_done, n * 9 + 5)
                        nc.vector.scalar_tensor_tensor(out=msq[:, p, :], in0=mdif[:, p, :], scalar=0.25, in1=mdif[:, p, :],
                                                       op0=ALU.mult, op1=ALU.mult).then_inc(small_done, 1)
                        dve.wait_ge(small_done, n * 9 + 8)
                        nc.vector.scalar_tensor_tensor(out=var[:, p, :], in0=vsum[:, p, :], scalar=1.0 / D, in1=msq[:, p, :],
                                                       op0=ALU.mult, op1=ALU.add).then_inc(var_ready, 1)

                    def hidden_lo(m):
                        dve.wait_ge(a_hi, s * 2 + (m + 1))
                        nc.vector.scalar_tensor_tensor(out=at_lo[:, p, m, :], in0=psA[m][:, :], scalar=0.0,
                                                       in1=f32(at_hi[:, p, m, :]), op0=ALU.max,
                                                       op1=ALU.subtract).then_inc(a_lo, 1)
                    if live(s):
                        hidden_lo(0)
                    if live(s - 2):
                        n = s - 2
                        dve.wait_ge(dev_ready, n + 1)
                        nc.vector.reciprocal(rstd[:, p, :], dev[:, p, :]).then_inc(small_done, 1)
                        dve.wait_ge(small_done, n * 9 + 9)
                        nc.vector.scalar_tensor_tensor(out=nmr[:, p, :], in0=msum[:, p, :], scalar=-0.5, in1=rstd[:, p, :],
                                                       op0=ALU.mult, op1=ALU.mult).then_inc(rstd_ready, 1)
                    if live(s):
                        hidden_lo(1)
                    if live(s + 2):
                        if live(s):
                            dve.wait_ge(t_done, (s + 1) * 2)
                        for w in range(W):
                            ins = nc.vector.tensor_scalar(hot[:, p, w, :, 0:WP[w]], c["iota"][:, :, 0:WP[w]],
                                                          c["key"][:, ds((s + 2) * W + w, 1)], None, ALU.is_equal)
                        ins.then_inc(hot_ready, 1)
                    if live(s + 1):
                        for k in range(2):
                            dve.wait_ge(t_hi, (s + 1) * 2 + (k + 1))
                            nc.vector.tensor_tensor(ht_lo[:, q, k, :], psT[k][:, :], f32(ht_hi[:, q, k, :]),
                                                    ALU.subtract).then_inc(t_lo, 1)
                    if live(s - 1):
                        dve.wait_ge(b_done, s)
                        dve.wait_ge(x_loaded[q], count_of(s - 1, q))
                        if live(s - 3):
                            dve.wait_ge(x_stored[q], count_of(s - 3, q))
                            dve.wait_ge(normed, s - 2)
                        nc.vector.tensor_tensor(flat(xs[:, q, :, :]), psB[:, :], flat(xr[:, q, :, :]), ALU.add).then_inc(x_ready, 1)
                        dve.wait_ge(x_ready, s)
                    if live(s - 2):
                        dve.wait_ge(h_hi, s - 1)
                        nc.vector.tensor_tensor(hnt_lo[:, p, :], psH[:, :], f32(hnt_hi[:, p, :]), ALU.subtract).then_inc(h_lo, 1)
                run_pipeline(dve, sh, step, -2, S + 2)

            @block.scalar
            def _(act):
                def step(s, p):
                    q = 1 - p

                    def hidden_hi(m):
                        act.wait_ge(a_done, s * 2 + (m + 1))
                        if live(s - 2) and m == 0:
                            act.wait_ge(b_done, s - 1)
                        nc.scalar.activation(at_hi[:, p, m, :], psA[m][:, :], ACT.Relu).then_inc(a_hi, 1)
                    if live(s):
                        hidden_hi(0)
                    if live(s - 2):
                        act.wait_ge(var_ready, s - 1)
                        nc.scalar.activation(dev[:, p, :], var[:, p, :], ACT.Sqrt, bias=c["eps"][:, :]).then_inc(dev_ready, 1)
                    if live(s):
                        hidden_hi(1)
                    if live(s - 2):
                        act.wait_ge(rstd_ready, s - 1)
                        if live(s - 4):
                            act.wait_ge(h_done, s - 3)
                        for t in range(T):
                            ins = nc.scalar.activation(hn[:, p, t, :], xs[:, p, t, :], ACT.Relu,
                                                       bias=nmr[:, p, t:t + 1], scale=rstd[:, p, t:t + 1])
                        ins.then_inc(normed, 1)
                    if live(s - 3):
                        act.wait_ge(y_done, s - 2)
                        if live(s - 5):
                            act.wait_ge(y_stored[q], count_of(s - 5, q))
                        for t in range(T):
                            ins = nc.scalar.activation(yo[:, q, t, :], psY[:, t * D:(t + 1) * D], ACT.Copy,
                                                       scale=c["rsdeg"][:, ds((s - 3) * T + t, 1)])
                        ins.then_inc(y_read, 1)
                    if live(s + 1):
                        for k in range(2):
                            act.wait_ge(t_done, (s + 1) * 2 + (k + 1))
                            if live(s - 1) and k == 0:
                                act.wait_ge(a_done, s * 2)
                            nc.scalar.activation(ht_hi[:, q, k, :], psT[k][:, :], ACT.Copy).then_inc(t_hi, 1)
                    if live(s + 2):
                        act.wait_ge(gath_loaded[p], count_of(s + 2, p) * W)
                        if live(s):
                            act.wait_ge(t_done, (s + 1) * 2)
                        nc.scalar.activation(gat_hi[:, p, :, :], gat[:, p, :, :], ACT.Copy).then_inc(gath_hi, 1)
                    if live(s - 2):
                        act.wait_ge(h_done, s - 1)
                        if live(s - 4):
                            act.wait_ge(y_done, s - 3)
                        nc.scalar.activation(hnt_hi[:, p, :], psH[:, :], ACT.Copy).then_inc(h_hi, 1)
                run_pipeline(act, sh, step, -2, S + 2)

            @block.tensor
            def _(pe):
                def step(s, p):
                    q = 1 - p
                    if live(s):
                        pe.wait_ge(t_lo, (s + 1) * 2)
                        if live(s - 1):
                            pe.wait_ge(a_lo, s * 2)
                        for m in range(2):
                            nc.tensor.matmul(psA[m][:, :], bias_parts(c, "b2a", m * P, (m + 1) * P), c["ones3"][:, :],
                                             start=True, stop=False)
                            for k in range(2):
                                ins = product(nc, psA[m][:, :], *weight(c, "w2a", k, m * P, (m + 1) * P),
                                              ht_hi[:, p, k, :], ht_lo[:, p, k, :], False, k == 1)
                            ins.then_inc(a_done, 1)
                    if live(s - 3):
                        pe.wait_ge(h_lo, s - 2)
                        if live(s - 4):
                            pe.wait_ge(y_read, s - 3)
                        for t in range(T):
                            ins = product(nc, psY[:, t * D:(t + 1) * D], hnt_hi[:, q, t * P:(t + 1) * P],
                                          hnt_lo[:, q, t * P:(t + 1) * P], *weight(c, "wg1", 0), t == 0, t == T - 1)
                        ins.then_inc(y_done, 1)
                    if live(s + 1):
                        pe.wait_ge(own_loaded[q], count_of(s + 1, q))
                        pe.wait_ge(gath_lo, s + 2)
                        pe.wait_ge(hot_ready, s + 2)
                        if live(s):
                            pe.wait_ge(t_lo, (s + 1) * 2)
                        for k in range(2):
                            for t in range(T):
                                nc.tensor.matmul(psT[k][:, t * P:(t + 1) * P], own[:, q, t, k * P:(k + 1) * P],
                                                 c["ident"][:, :], is_transpose=True, start=t == 0, stop=False)
                            for w in range(W):
                                for rows in (gat_lo, gat_hi):
                                    ins = nc.tensor.matmul(windows(psT[k][:, :])[:, :, W0[w]:W0[w] + WP[w]],
                                                           rows[:, q, w, k * P:(k + 1) * P], hot[:, q, w, :, 0:WP[w]],
                                                           start=False, stop=w == W - 1 and rows is gat_hi)
                            ins.then_inc(t_done, 1)
                    if live(s - 1):
                        pe.wait_ge(a_lo, s * 2)
                        if live(s - 2):
                            pe.wait_ge(x_ready, s - 1)
                        for t in range(T):
                            acc = psB[:, t * D:(t + 1) * D]
                            nc.tensor.matmul(acc, c["ones3"][:, 0:P], bias_parts(c, "b2b", 0, D), start=t == 0, stop=False)
                            for k in range(2):
                                rows = at_hi[:, q, k, t * P:(t + 1) * P], at_lo[:, q, k, t * P:(t + 1) * P]
                                ins = product(nc, acc, *rows, *weight(c, "w2b", k), False, t == T - 1 and k == 1)
                        ins.then_inc(b_done, 1)
                    if live(s - 2):
                        pe.wait_ge(normed, s - 1)
                        if live(s - 3):
                            pe.wait_ge(h_lo, s - 2)
                        for t in range(T):
                            ins = nc.tensor.matmul(psH[:, t * P:(t + 1) * P], hn[:, p, t, :], c["ident"][:, :],
                                                   is_transpose=True, start=t == 0, stop=t == T - 1)
                        ins.then_inc(h_done, 1)
                run_pipeline(pe, sh, step, -1, S + 2)


def gcn(nc, sh, c, tables, tag, y, bias, out, final):
    S = sh.S
    live = lambda s: not isinstance(s, int) or 0 <= s < S
    x1 = tables["x1"]
    with ExitStack() as ctx:
        sb = lambda name, shape, dt=F32: ctx.enter_context(nc.sbuf_tensor(f"{tag}_{name}", shape, dt))
        ps = lambda name: ctx.enter_context(nc.psum_tensor(f"{tag}_{name}", [P, 512], F32))
        sem = lambda name: ctx.enter_context(nc.semaphore(f"{tag}_{name}"))
        K = 4
        own = sb("own", [P, K, T, D])
        shifted = sb("shifted", [P, 2, T, D])
        gat = sb("gat", [P, K, W, D])
        ix = sb("ix", [P, K, W], I32)
        hot = sb("hot", [P, 2, W, T, WP[0]])
        rt = sb("rt", [P, 2, R], F32 if final else F32R)
        rt_lo = sb("rt_lo", [P, 2, R], F32R)
        xs = sb("xs", [P, K, T, D])
        res = sb("res", [P, 2, T, D])
        psT = [ps("psT0"), ps("psT1")]
        psY = [ps("psY0"), ps("psY1")]
        own_loaded = [sem(f"own_loaded{i}") for i in range(K)]
        gath_loaded = [sem(f"gath_loaded{i}") for i in range(K)]
        x_loaded = [sem(f"x_loaded{i}") for i in range(K)]
        stored = [sem("stored0"), sem("stored1")]
        ix_ready, ready, t_done, t_hi, y_done, y_read = (sem("ix_ready"), sem("ready"), sem("t_done"), sem("t_hi"),
                                                         sem("y_done"), sem("y_read"))
        t_lo = sem("t_lo")
        t_read = t_hi if final else t_lo

        with nc.Block() as block:
            @block.sync
            def _(sp):
                def body(table):
                    def step(s, p):
                        if live(s + 4):
                            if live(s):
                                hold(sp, ready, s + 1, c["sp_passed"])
                            sp.dma_start(flat(own[:, p, :, :]), node_rows(table, s + 4, D)).then_inc(own_loaded[p], 16)
                        if final and live(s + 3):
                            if live(s - 1):
                                hold(sp, y_read, s, c["sp_passed"])
                            sp.dma_start(flat(xs[:, (p + 3) % K, :, :]), node_rows(x1, s + 3, D)
                                         ).then_inc(x_loaded[(p + 3) % K], 16)
                        if live(s - 1):
                            q = (p + 1) % 2
                            if not final:
                                hold(sp, y_read, s, c["sp_passed"])
                            if final and isinstance(s, int) and s == S:
                                rows = out[(S - 1) * R:sh.N, :].rearrange("(p t) f -> p (t f)", t=T)
                                frm = flat(res[0:sh.LAST, q, :, :])
                            else:
                                rows, frm = node_rows(out, s - 1, D), flat(res[:, q, :, :])
                            if final and not live(s + 3):
                                hold(sp, y_read, s, c["sp_passed"])
                            sp.dma_start(rows, frm).then_inc(stored[q], 16)
                    run_pipeline(sp, sh, step, -4, S, K)
                load_own(sp, sh, c, y, tables["sum128"], body)
                sp.wait_ge(stored[0], 8 * S)
                sp.wait_ge(stored[1], 8 * S)

            @block.gpsimd
            def _(pool):
                def copy_ix(s, q):
                    pool.tensor_copy(ix[:, q, :], c["idx"][:, ds(s * W, W)]).then_inc(ix_ready, 1)

                def step(s, p):
                    if live(s + 4):
                        if live(s):
                            hold(pool, t_done, s + 1, c["pool_passed"])
                        hold(pool, ix_ready, s + 5, c["pool_passed"])
                        for w in range(W):
                            pool.indirect_dma_start(gat[:, p, w, :], None, y,
                                                    bass.IndirectOffsetOnAxis(ap=ix[:, p, w:w + 1], axis=0)
                                                    ).then_inc(gath_loaded[p], 16)
                    if live(s + 5):
                        q = (p + 1) % K
                        if live(s + 1):
                            hold(pool, gath_loaded[q], count_of(s + 1, q, K) * W, c["pool_passed"])
                        copy_ix(s + 5, q)
                copy_ix(0, 0)
                run_pipeline(pool, sh, step, -4, S, K)

            @block.vector
            def _(dve):
                def step(s, p):
                    r, p, q = p, p % 2, (p + 1) % 2
                    if live(s + 2):
                        r2 = (r + 2) % K
                        dve.wait_ge(own_loaded[r2], count_of(s + 2, r2, K))
                        if live(s):
                            dve.wait_ge(t_done, s + 1)
                        for t in range(T):
                            nc.vector.scalar_tensor_tensor(out=shifted[:, p, t, :], in0=bias[:, :],
                                                           scalar=c["sqdeg"][:, ds((s + 2) * T + t, 1)],
                                                           in1=own[:, r2, t, :], op0=ALU.mult, op1=ALU.add)
                        for w in range(W):
                            ins = nc.vector.tensor_scalar(hot[:, p, w, :, 0:WP[w]], c["iota"][:, :, 0:WP[w]],
                                                          c["key"][:, ds((s + 2) * W + w, 1)], None, ALU.is_equal)
                        ins.then_inc(ready, 1)
                    if live(s + 1) and not final:
                        dve.wait_ge(t_hi, s + 2)
                        nc.vector.scalar_tensor_tensor(out=rt_lo[:, q, :], in0=psT[q][:, :], scalar=0.0,
                                                       in1=f32(rt[:, q, :]), op0=ALU.max, op1=ALU.subtract).then_inc(t_lo, 1)
                    if live(s):
                        dve.wait_ge(y_done, s + 1)
                        if live(s - 2):
                            dve.wait_ge(stored[p], count_of(s - 2, p))
                        if final:
                            dve.wait_ge(x_loaded[r], count_of(s, r, K))
                            for t in range(T):
                                ins = nc.vector.scalar_tensor_tensor(out=res[:, p, t, :], in0=psY[p][:, t * D:(t + 1) * D],
                                                                     scalar=c["rsdeg"][:, ds(s * T + t, 1)],
                                                                     in1=xs[:, r, t, :], op0=ALU.mult, op1=ALU.add)
                        else:
                            ins = nc.vector.tensor_tensor(res[:, p, :, :], psY[p][:, :].rearrange("p (t f) -> p t f", t=T),
                                                          wide(c["rdeg"][:, ds(s * T, T)], D), ALU.mult)
                        ins.then_inc(y_read, 1)
                run_pipeline(dve, sh, step, -2, S, K)

            @block.scalar
            def _(act):
                def step(s, p):
                    q = 1 - p
                    if live(s + 1):
                        act.wait_ge(t_done, s + 2)
                        if live(s - 1):
                            act.wait_ge(y_done, s)
                        nc.scalar.activation(rt[:, q, :], psT[q][:, :], ACT.Relu).then_inc(t_hi, 1)
                run_pipeline(act, sh, step, -1, S)

            @block.tensor
            def _(pe):
                def step(s, p):
                    r1, p, q = (p + 1) % K, p % 2, (p + 1) % 2
                    if live(s + 1):
                        pe.wait_ge(gath_loaded[r1], count_of(s + 1, r1, K) * W)
                        pe.wait_ge(ready, s + 2)
                        if live(s - 1):
                            pe.wait_ge(t_read, s)
                        for t in range(T):
                            nc.tensor.matmul(psT[q][:, t * P:(t + 1) * P], shifted[:, q, t, :], c["ident"][:, :],
                                             is_transpose=True, start=t == 0, stop=False)
                        for w in range(W):
                            ins = nc.tensor.matmul(windows(psT[q][:, :])[:, :, W0[w]:W0[w] + WP[w]], gat[:, r1, w, :],
                                                   hot[:, q, w, :, 0:WP[w]], start=False, stop=w == W - 1)
                        ins.then_inc(t_done, 1)
                    if live(s):
                        pe.wait_ge(t_read, s + 1)
                        if live(s - 2):
                            pe.wait_ge(y_read, s - 1)
                        for t in range(T):
                            acc, lhs = psY[p][:, t * D:(t + 1) * D], rt[:, p, t * P:(t + 1) * P]
                            if final:
                                ins = nc.tensor.matmul(acc, lhs, c["ident"][:, :], is_transpose=True,
                                                       start=t == 0, stop=t == T - 1)
                            else:
                                ins = product(nc, acc, lhs, rt_lo[:, p, t * P:(t + 1) * P], *weight(c, "wg2", 0),
                                              t == 0, t == T - 1)
                        ins.then_inc(y_done, 1)
                run_pipeline(pe, sh, step, -1, S, K)


_INS = ['x', 'src', 'dst', 'L0_gnn_W1a', 'L0_gnn_b1a', 'L0_gnn_W1b', 'L0_gnn_b1b', 'L0_gnn_W2a', 'L0_gnn_b2a',
        'L0_gnn_W2b', 'L0_gnn_b2b', 'L1_gnn_W1', 'L1_gnn_b1', 'L1_gnn_W2', 'L1_gnn_b2']


def kernel(**inputs):
    import numpy as _np
    import concourse.bacc as _bacc
    from concourse import mybir as _mybir
    from concourse.bass_utils import run_bass_kernel_spmd as _run

    nc = _bacc.Bacc("TRN2", target_bir_lowering=False, num_devices=1)
    arrays, args = {}, []
    for name in _INS:
        a = _np.ascontiguousarray(inputs[name])
        arrays[f"in_{name}_dram"] = a
        args.append(nc.dram_tensor(f"in_{name}_dram", a.shape, _mybir.dt.from_np(a.dtype), kind="ExternalInput").ap())
    out = nc.dram_tensor("out_0_dram", inputs["x"].shape, _mybir.dt.float32, kind="ExternalOutput").ap()
    graph_kernel(nc, *args, out)
    r = _run(nc, [arrays], core_ids=[0])
    return r.results[0]["out_0_dram"]
```

```python
import concourse.bass as bass
from concourse import mybir
from contextlib import ExitStack


F32, BF16, F16, I32 = mybir.dt.float32, mybir.dt.bfloat16, mybir.dt.float16, mybir.dt.int32
F32R = mybir.dt.float32r
ALU = mybir.AluOpType
ACT = mybir.ActivationFunctionType
AXX = mybir.AxisListType.X

P = 128
T = 4
R = P * T
W = 3
WP = [44, 44, 40]
W0 = [0, 44, 88]
D, DH = 128, 256
EPS = 1e-5
FAR = 1 << 20
START = 6


def ds(start, size):
    return bass.ds(start, size)


def product(nc, acc, hi, lo, moving_hi, moving_lo, start, stop):
    nc.tensor.matmul(acc, lo, moving_hi, start=start, stop=False)
    nc.tensor.matmul(acc, hi, moving_lo, start=False, stop=False)
    return nc.tensor.matmul(acc, hi, moving_hi, start=False, stop=stop)


W_AT, W_COLS = {}, 0
for _name, _k, _n in (("w1a", 1, DH), ("w1b", 2, DH), ("w2a", 2, DH), ("w2b", 2, D), ("wg1", 1, D), ("wg2", 1, D)):
    W_AT[_name] = (W_COLS, _n)
    W_COLS += _k * _n
BIAS_AT, BIAS_COLS = {}, 0
for _name, _n in (("b1b", DH), ("b1a", DH), ("b2a", DH)):
    BIAS_AT[_name] = BIAS_COLS
    BIAS_COLS += _n


def weight(c, name, k, lo=0, hi=None):
    at, n = W_AT[name]
    cols = slice(at + k * n + lo, at + k * n + (n if hi is None else hi))
    return c["w_hi"][:, cols], c["w_lo"][:, cols]


def bias_parts(c, name, lo, hi):
    return c["bias3"][:, BIAS_AT[name] + lo:BIAS_AT[name] + hi]


def f32(ap):
    return ap.bitcast(F32)


class Shapes:
    def __init__(self, n, e):
        self.N, self.E = n, e
        self.S = -(-n // R)
        self.S += self.S % 2
        self.NP = self.S * R
        self.LAST = (n - (self.S - 1) * R) // T
        assert n % T == 0 and self.LAST > 0 and self.S >= START + 12
        self.NB = -(-self.S // P)
        while self.S % self.NB:
            self.NB += 1
        self.SB = self.S // self.NB
        self.EP = max(k for k in range(1, P + 1) if e % k == 0)
        self.EC = e // self.EP
        self.ER = -(-e // P)
        assert self.EC % 8 == 0 and self.EC > 16 and e % P


def hold(engine, sem, value, passed):
    engine.wait_ge(sem, value)
    if not isinstance(value, int):
        engine.sem_inc(passed, 1)


def count_of(s, p, slots=2):
    return (s - p) * (16 // slots) + 16


def run_pipeline(engine, sh, step, first, last, slots=2):
    start = -(-START // slots) * slots
    stop = start + (sh.S - 3 - slots // 2 - start) // slots * slots
    for s in range(first, start):
        step(s, s % slots)
    with engine.Fori(start, stop - slots + 1, slots) as i:
        for p in range(slots):
            step(i + p, p)
    for s in range(stop, last + 1):
        step(s, s % slots)


def node_rows(table, s, f):
    return table[ds(s * R, R), 0:f].rearrange("(p t) f -> p (t f)", t=T)


def flat(ap):
    return ap.rearrange("p t f -> p (t f)")


def windows(ap):
    return ap.rearrange("p (t q) -> p t q", t=T)


def wide(ap, n):
    return ap.unsqueeze(2).to_broadcast([ap.shape[0], ap.shape[1], n])


def graph_kernel(nc, x, src, dst, w1a, b1a, w1b, b1b, w2a, b2a, w2b, b2b, wg1, bg1, wg2, bg2, out):
    sh = Shapes(x.shape[0], src.shape[0])
    with ExitStack() as ctx:
        sb = lambda name, shape, dt=F32: ctx.enter_context(nc.sbuf_tensor(name, shape, dt))
        tables = {
            "h1": nc.dram_tensor("h1", (sh.NP, DH), F32).ap(),
            "g1": nc.dram_tensor("g1_rows", (sh.NP, D), F32).ap(),
            "g2": nc.dram_tensor("g2_rows", (sh.NP, D), F32).ap(),
            "x1": nc.dram_tensor("x1", (sh.NP, D), F32).ap(),
            "sum128": nc.dram_tensor("sum128", (sh.NP + P, D), F32).ap(),
            "sum256": nc.dram_tensor("sum256", (sh.NP + P, DH), F32).ap(),
            "edges": nc.dram_tensor("edges", (sh.ER + 1, 2 * P), I32).ap(),
        }
        c = {
            "ident": sb("ident", [P, P]),
            "iota": sb("iota", [P, T, WP[0]], F16),
            "eps": sb("eps", [P, 1]),
            "ones3": sb("ones3", [P, R], BF16),
            "bias3": sb("bias3", [P, BIAS_COLS], BF16),
            "w_hi": sb("w_hi", [P, W_COLS], F32R),
            "w_lo": sb("w_lo", [P, W_COLS], F32R),
            "b2b": sb("b2b_sb", [P, 1]),
            "bg1": sb("bg1_sb", [P, D]),
            "bg2": sb("bg2_sb", [P, D]),
            "idx": sb("idx", [P, sh.S * W], I32),
            "key": sb("key", [P, sh.S * W]),
            "rsdeg": sb("rsdeg", [P, sh.S * T]),
            "sp_passed": ctx.enter_context(nc.semaphore("sp_passed")),
            "pool_passed": ctx.enter_context(nc.semaphore("pool_passed")),
            "flag": sb("flag_f", [P, 2]),
            "flag_int": sb("flag_int", [P, 1], I32),
        }
        prepare(nc, sh, c, tables, src, dst, dict(w1a=w1a, w1b=w1b, w2a=w2a, w2b=w2b, wg1=wg1, wg2=wg2,
                                                  b1a=b1a, b2a=b2a, b1b=b1b, b2b=b2b, bg1=bg1, bg2=bg2))
        general_pass(nc, sh, c, tables, "g1", x, tables["sum128"], D, normed=True)
        gin_first(nc, sh, c, tables, x)
        general_pass(nc, sh, c, tables, "g2", tables["h1"], tables["sum256"], DH, normed=False)
        gin_second(nc, sh, c, tables, x)
        general_pass(nc, sh, c, tables, "g3", tables["g1"], tables["sum128"], D, normed=False)
        gcn(nc, sh, c, tables, "c1", tables["g1"], "wg1", c["bg1"], out=tables["g2"], final=False)
        general_pass(nc, sh, c, tables, "g4", tables["g2"], tables["sum128"], D, normed=False)
        gcn(nc, sh, c, tables, "c2", tables["g2"], "wg2", c["bg2"], out=out, final=True)


def prepare(nc, sh, c, tables, src, dst, given):
    S, SB, NB, EP, EC = sh.S, sh.SB, sh.NB, sh.EP, sh.EC
    G = NB * W
    NCOL = S * T
    edges = tables["edges"]
    full, rest = sh.E // P, sh.E % P
    SPLITS = [(a, min(a + 512, NCOL)) for a in range(0, NCOL, 512)]
    D_COUNTS = 5 + len(SPLITS) + 2
    D_DEG = D_COUNTS + 1
    D_TOT = D_DEG + 3
    D_ROWS = D_TOT + 6
    D_MATCHED = D_ROWS + 11 + 7 * (1 + G) + G + 1 + W + 1
    D_KEYS = D_MATCHED + 3
    with ExitStack() as ctx:
        sb = lambda name, shape, dt=F32: ctx.enter_context(nc.sbuf_tensor(name, shape, dt))
        ps = lambda name: ctx.enter_context(nc.psum_tensor(name, [P, 512], F32))
        sem = lambda name: ctx.enter_context(nc.semaphore(name))
        dsti = sb("dsti", [EP, EC], I32)
        part_i = sb("part_i", [EP, EC], I32)
        colh_i = sb("colh_i", [EP, EC], I32)
        coll_i = sb("coll_i", [EP, EC], I32)
        part_f = sb("part_f", [EP, EC])
        col_f = sb("col_f", [EP, EC])
        iota_p = sb("iota_p", [EP, P], F16)
        iota_c = sb("iota_c", [EP, NCOL], F16)
        diff_p = sb("diff_p", [EP, 8, P], BF16)
        dist_p = sb("dist_p", [EP, 8, P], BF16)
        hot_p = sb("hot_p", [EP, 8, P], BF16)
        hot_c = sb("hot_c", [EP, 8, NCOL], BF16)
        counts = sb("counts", [P, NCOL])
        deg = sb("deg", [P, NCOL])
        sqdeg = sb("sqdeg", [P, NCOL])
        rs0 = sb("rs0", [P, NCOL])
        mask_v = sb("mask_v", [P, W])
        mask_lo = sb("mask_lo", [P, W])
        mask = sb("mask", [P, W])
        tri = sb("tri", [SB, SB])
        ones = sb("ones", [P, P])
        cw = sb("cw", [SB, NB, W])
        two = sb("two", [SB, NB])
        tot = sb("tot", [SB, NB])
        starts = sb("starts", [SB, NB, W])
        starts_i = sb("starts_i", [SB, G], I32)
        rows_i = sb("rows_i", [SB, 2, G], I32)
        bits_i = sb("bits_i", [SB, 7, G], I32)
        bits = sb("bits", [SB, 7, G])
        base_i = sb("base_i", [SB, NB, W], I32)
        base = sb("base", [SB, G])
        got = sb("got", [SB, G, 2, 2 * P], I32)
        runs = sb("runs", [SB, G, 2, 2 * P])
        diff = sb("diff", [SB, G, 2, 2 * P])
        runs_b = sb("runs_b", [SB, G, 2, 2 * P])
        keys = sb("keys", [SB, G, P])
        in_lo = sb("in_lo", [SB, G, P])
        in_win = sb("in_win", [SB, G, P])
        matched = sb("matched", [SB, 1])
        pad_src = sb("pad_src", [1, P], I32)
        pad_dst = sb("pad_dst", [1, P], I32)
        brow = sb("brow", [1, BIAS_COLS])
        bres = sb("bres", [1, 2, BIAS_COLS])
        bpart = sb("bpart", [1, 3, BIAS_COLS], BF16)
        w_all = sb("w_all", [P, W_COLS])
        bank = [ps(f"pb{i}") for i in range(6)]
        consts = sem("p_consts")
        edges_in, pad_in, weights_in = sem("p_edges_in"), sem("p_pad_in"), sem("p_weights_in")
        dst_in, edges_done, rows_got = sem("p_dst_in"), sem("p_edges_done"), sem("p_rows_got")
        hot_ready, counted, d, a, pe_done = sem("p_hot"), sem("p_counted"), sem("p_dve"), sem("p_act"), sem("p_pe")
        bias_row_in, bias_split, bias_in = sem("p_bias_row"), sem("p_bias_split"), sem("p_bias_in")
        w_split = sem("p_w_split")
        diff_p_ready, dist_p_ready, hot_p_ready = sem("p_diff_p"), sem("p_dist_p"), sem("p_hot_p")
        n_consts = [0]

        with nc.Block() as block:
            @block.gpsimd
            def _(pool):
                def made(ins):
                    n_consts[0] += 1
                    ins.then_inc(consts, 1)
                made(pool.iota(iota_p[:, :], pattern=[[1, P]], base=0, channel_multiplier=0,
                               allow_small_or_imprecise_dtypes=True))
                made(pool.iota(iota_c[:, :], pattern=[[1, NCOL]], base=0, channel_multiplier=0,
                               allow_small_or_imprecise_dtypes=True))
                made(pool.memset(pad_src[:, :], 0))
                made(pool.memset(pad_dst[:, :], FAR))
                made(pool.memset(c["ident"][:, :], 0.0))
                made(pool.memset(tri[:, :], 0.0))
                made(pool.memset(ones[:, :], 1.0))
                made(pool.memset(c["ones3"][:, :], 1.0))
                made(pool.memset(c["bias3"][:, :], 0.0))
                made(pool.memset(c["eps"][:, :], EPS))
                made(pool.iota(c["iota"][:, :, :], pattern=[[1, T], [T, WP[0]]], base=0, channel_multiplier=0,
                               allow_small_or_imprecise_dtypes=True))
                made(pool.iota(mask_v[:, :], pattern=[[-WP[0], W]], base=0, channel_multiplier=1,
                               allow_small_or_imprecise_dtypes=True))
                for b in range(NB):
                    made(pool.iota(base_i[:, b, :], pattern=[[T * WP[0], W]], base=b * SB * R,
                                   channel_multiplier=R))
                pool.wait_ge(consts, n_consts[0])
                made(pool.affine_select(out=c["ident"][:, :], in_=c["ident"][:, :], compare_op=ALU.not_equal,
                                        fill=1.0, base=0, pattern=[[-1, P]], channel_multiplier=1))
                made(pool.affine_select(out=tri[:, :], in_=tri[:, :], compare_op=ALU.is_ge,
                                        fill=1.0, base=0, pattern=[[-1, SB]], channel_multiplier=1))

                def diff_group(i, h):
                    pool.tensor_tensor(diff_p[:, h:h + 4, :], iota_p[:, :].unsqueeze(1).to_broadcast([EP, 4, P]),
                                       wide(part_f[:, ds(i, 4)], P), ALU.subtract).then_inc(diff_p_ready, 4)
                pool.wait_ge(d, 5)
                diff_group(0, 0)
                diff_group(4, 4)
                with pool.Fori(8, EC - 7, 8) as i:
                    for h in (0, 4):
                        hold(pool, dist_p_ready, i + (h - 4), c["pool_passed"])
                        diff_group(i + h, h)
                pool.wait_ge(edges_done, 16)
                pool.wait_ge(d, D_ROWS)
                for g in range(G):
                    for r in range(2):
                        pool.indirect_dma_start(got[:, g, r, :], None, edges,
                                                bass.IndirectOffsetOnAxis(ap=rows_i[:, r, g:g + 1], axis=0)
                                                ).then_inc(rows_got, 16)

            @block.sync
            def _(sp):
                sp.dma_start(dsti[:, :], dst.rearrange("(p c) -> p c", p=EP)).then_inc(dst_in, 16)
                n = 0
                for kind, given_list in enumerate((src, dst)):
                    lane = slice(kind * P, (kind + 1) * P)
                    sp.dma_start(edges[0:full, lane],
                                 given_list[0:full * P].rearrange("(r c) -> r c", c=P)).then_inc(edges_in, 16)
                    sp.dma_start(edges[full:full + 1, kind * P:kind * P + rest],
                                 given_list[full * P:sh.E].rearrange("(r c) -> r c", r=1)).then_inc(edges_in, 16)
                    n += 2
                sp.wait_ge(consts, 4)
                for kind, pad in enumerate((pad_src, pad_dst)):
                    sp.dma_start(edges[full:full + 1, kind * P + rest:(kind + 1) * P],
                                 pad[:, 0:P - rest]).then_inc(pad_in, 16)
                    sp.dma_start(edges[full + 1:full + 2, kind * P:(kind + 1) * P], pad[:, :]).then_inc(pad_in, 16)
                sp.wait_ge(edges_in, 16 * n)
                sp.wait_ge(pad_in, 64)
                sp.sem_inc(edges_done, 16)

            @block.scalar
            def _(act):
                for name, at in BIAS_AT.items():
                    act.dma_start(brow[:, at:at + given[name].shape[0]],
                                  given[name].rearrange("(r c) -> r c", r=1)).then_inc(bias_row_in, 16)
                loads = [
                    (c["b2b"][:, :], given["b2b"].rearrange("(p o) -> p o", o=1)),
                    (c["bg1"][:, :], given["bg1"].partition_broadcast(P)),
                    (c["bg2"][:, :], given["bg2"].partition_broadcast(P)),
                ]
                for name, (at, n) in W_AT.items():
                    k = given[name].shape[0] // P
                    loads.append((w_all[:, at:at + k * n].rearrange("p (k n) -> p k n", k=k),
                                  given[name].rearrange("(k p) n -> p k n", p=P)))
                for to, frm in loads:
                    act.dma_start(to, frm).then_inc(weights_in, 16)

                def hot_group(i, h):
                    act.wait_ge(diff_p_ready, i + 4)
                    nc.scalar.activation(dist_p[:, h:h + 4, :], diff_p[:, h:h + 4, :], ACT.Abs).then_inc(dist_p_ready, 4)
                    act.wait_ge(dist_p_ready, i + 4)
                    nc.scalar.activation(hot_p[:, h:h + 4, :], dist_p[:, h:h + 4, :], ACT.Relu, scale=-1.0,
                                         bias=1.0).then_inc(hot_p_ready, 4)
                hot_group(0, 0)
                hot_group(4, 4)
                with act.Fori(8, EC - 7, 8) as i:
                    for h in (0, 4):
                        act.wait_ge(counted, i + (h - 4))
                        hot_group(i + h, h)
                act.wait_ge(weights_in, 16 * len(loads))
                nc.scalar.activation(c["w_hi"][:, :], w_all[:, :], ACT.Copy).then_inc(w_split, 1)
                act.wait_ge(bias_split, 5)
                act.wait_ge(consts, n_consts[0])
                act.dma_start(c["bias3"][0:3, :], bpart[0:1, :, :]).then_inc(bias_in, 16)
                act.wait_ge(d, D_DEG)
                nc.scalar.activation(sqdeg[:, :], deg[:, :], ACT.Sqrt).then_inc(a, 1)
                act.wait_ge(bias_in, 16)

            @block.tensor
            def _(pe):
                def count_step(u, first, last):
                    for n, (lo, hi) in enumerate(SPLITS):
                        ins = nc.tensor.matmul(bank[n][:, 0:hi - lo], hot_p[:, u, :], hot_c[:, u, lo:hi],
                                               start=first, stop=last)
                    ins.then_inc(counted, 1)
                def count_turn(i, first, last):
                    for u in range(8):
                        if u % 4 == 0:
                            pe.wait_ge(hot_p_ready, i + (u + 4))
                        pe.wait_ge(hot_ready, i + (u + 1))
                        count_step(u, first and u == 0, last and u == 7)
                count_turn(0, True, False)
                with pe.Fori(8, EC - 15, 8) as i:
                    count_turn(i, False, False)
                count_turn(EC - 8, False, True)
                pe.wait_ge(d, D_COUNTS)
                for b in range(NB):
                    for t in range(T):
                        ins = nc.tensor.matmul(bank[2][0:SB, b * W:(b + 1) * W],
                                               counts[:, b * SB * T + t:(b + 1) * SB * T:T], mask[:, :],
                                               start=t == 0, stop=t == T - 1)
                ins.then_inc(pe_done, 1)
                pe.wait_ge(d, D_TOT)
                for b in range(NB):
                    for bb in range(b + 1):
                        ins = nc.tensor.matmul(bank[3][0:SB, b:b + 1], tri[:, :] if bb == b else ones[0:SB, 0:SB],
                                               tot[:, bb:bb + 1], start=bb == 0, stop=bb == b)
                ins.then_inc(pe_done, 1)
                pe.wait_ge(d, D_MATCHED)
                nc.tensor.matmul(bank[3][:, 8:9], ones[0:SB, :], matched[:, :], start=True, stop=True).then_inc(pe_done, 1)
                for g in range(G):
                    nc.tensor.matmul(bank[4 + g // W % 2][:, (g % W) * P:(g % W) * P + SB], runs_b[:, g, 0, 0:P],
                                     c["ident"][0:SB, 0:SB], is_transpose=True, start=True, stop=True)
                    ins = nc.tensor.matmul(bank[g // W % 2][:, (g % W) * P:(g % W) * P + SB], keys[:, g, :],
                                           c["ident"][0:SB, 0:SB], is_transpose=True, start=True, stop=True)
                    if g % W == W - 1:
                        ins.then_inc(pe_done, 1)
                        if g < G - 1 and g // W >= 1:
                            pe.wait_ge(d, D_KEYS + 2 * W * (g // W))

            @block.vector
            def _(dve):
                at = [0]

                def link(ins, wait=True):
                    at[0] += 1
                    ins.then_inc(d, 1)
                    if wait:
                        dve.wait_ge(d, at[0])
                dve.wait_ge(dst_in, 16)
                link(nc.vector.tensor_scalar(part_i[:, :], dsti[:, :], 2, 127, ALU.logical_shift_right, ALU.bitwise_and), False)
                link(nc.vector.tensor_scalar(colh_i[:, :], dsti[:, :], 9, 2, ALU.logical_shift_right, ALU.logical_shift_left), False)
                link(nc.vector.tensor_scalar(coll_i[:, :], dsti[:, :], 3, None, ALU.bitwise_and))
                link(nc.vector.tensor_copy(part_f[:, :], part_i[:, :]), False)
                link(nc.vector.tensor_tensor(col_f[:, :], colh_i[:, :], coll_i[:, :], ALU.add))
                dve.wait_ge(consts, 2)

                def hot_step(i, u):
                    nc.vector.tensor_scalar(hot_c[:, u, :], iota_c[:, :], col_f[:, ds(i + u, 1)], None,
                                            ALU.is_equal).then_inc(hot_ready, 1)
                for u in range(8):
                    hot_step(0, u)
                with dve.Fori(8, EC - 7, 8) as i:
                    for u in range(8):
                        dve.wait_ge(counted, i + (u - 7))
                        hot_step(i, u)
                dve.wait_ge(counted, EC)
                for n, (lo, hi) in enumerate(SPLITS):
                    link(nc.vector.tensor_copy(counts[:, lo:hi], bank[n][:, 0:hi - lo]), False)
                dve.wait_ge(consts, n_consts[0])
                link(nc.vector.tensor_scalar(mask_lo[:, :], mask_v[:, :], 0.0, None, ALU.is_ge))
                link(nc.vector.scalar_tensor_tensor(out=mask[:, :], in0=mask_v[:, :], scalar=float(WP[0]),
                                                    in1=mask_lo[:, :], op0=ALU.is_lt, op1=ALU.mult))
                assert at[0] == D_COUNTS
                link(nc.vector.tensor_scalar(deg[:, :], counts[:, :], 1.0, None, ALU.add))
                assert at[0] == D_DEG
                dve.wait_ge(pe_done, 1)
                link(nc.vector.tensor_copy(cw[:, :, :], bank[2][0:SB, 0:G].rearrange("p (b w) -> p b w", w=W)))
                link(nc.vector.tensor_tensor(two[:, :], cw[:, :, 0], cw[:, :, 1], ALU.add))
                link(nc.vector.tensor_tensor(tot[:, :], two[:, :], cw[:, :, 2], ALU.add))
                assert at[0] == D_TOT
                dve.wait_ge(pe_done, 2)
                link(nc.vector.tensor_copy(starts[:, :, 0], bank[3][0:SB, 0:NB]))
                link(nc.vector.tensor_tensor(starts[:, :, 1], starts[:, :, 0], cw[:, :, 0], ALU.add), False)
                link(nc.vector.tensor_tensor(starts[:, :, 2], starts[:, :, 0], two[:, :], ALU.add))
                link(nc.vector.tensor_copy(starts_i[:, :], starts[:, :, :].rearrange("p b w -> p (b w)")))
                link(nc.vector.tensor_scalar(rows_i[:, 0, :], starts_i[:, :], 7, None, ALU.logical_shift_right))
                link(nc.vector.tensor_scalar(rows_i[:, 1, :], rows_i[:, 0, :], 1, None, ALU.add))
                assert at[0] == D_ROWS
                for k in range(7):
                    link(nc.vector.tensor_scalar(bits_i[:, k, :], starts_i[:, :], k, 1,
                                                 ALU.logical_shift_right, ALU.bitwise_and), k == 6)
                link(nc.vector.tensor_copy(bits[:, :, :], bits_i[:, :, :]), False)
                link(nc.vector.tensor_copy(base[:, :], base_i[:, :, :].rearrange("p b w -> p (b w)")), False)
                dve.wait_ge(rows_got, 16 * 2 * G)
                for r in range(2):
                    link(nc.vector.tensor_copy(runs[:, :, :, r * P:(r + 1) * P],
                                               got[:, :, r, :].rearrange("p g (k e) -> p g k e", k=2)), r == 1)
                now, then = runs, runs_b
                for k in range(6, -1, -1):
                    step = 1 << k
                    length = P + step - 1
                    link(nc.vector.tensor_tensor(diff[:, :, :, 0:length], now[:, :, :, step:step + length],
                                                 now[:, :, :, 0:length], ALU.subtract))
                    for g in range(G):
                        link(nc.vector.scalar_tensor_tensor(out=then[:, g, :, 0:length], in0=diff[:, g, :, 0:length],
                                                            scalar=bits[:, k, g:g + 1], in1=now[:, g, :, 0:length],
                                                            op0=ALU.mult, op1=ALU.add), g == G - 1)
                    now, then = then, now
                assert now is runs_b
                for g in range(G):
                    link(nc.vector.tensor_scalar(keys[:, g, :], now[:, g, 1, 0:P], base[:, g:g + 1], None,
                                                 ALU.subtract), g == G - 1)
                link(nc.vector.tensor_scalar(in_lo[:, :, :], keys[:, :, :], 0.0, None, ALU.is_ge))
                for w in range(W):
                    link(nc.vector.scalar_tensor_tensor(out=in_win[:, w::W, :], in0=keys[:, w::W, :],
                                                        scalar=float(T * WP[w]), in1=in_lo[:, w::W, :],
                                                        op0=ALU.is_lt, op1=ALU.mult), w == W - 1)
                link(nc.vector.reduce_sum(matched[:, :], in_win[:, :, :].rearrange("p g e -> p (g e)"), axis=AXX))
                assert at[0] == D_MATCHED
                dve.wait_ge(pe_done, 3)
                link(nc.vector.tensor_scalar(c["flag"][:, 0:1], bank[3][:, 8:9], float(sh.E), None, ALU.is_equal), False)
                link(nc.vector.tensor_scalar(c["flag"][:, 1:2], bank[3][:, 8:9], float(sh.E), None, ALU.not_equal))
                link(nc.vector.tensor_copy(c["flag_int"][:, :], c["flag"][:, 1:2]), False)
                assert at[0] == D_KEYS
                for b in range(NB):
                    dve.wait_ge(pe_done, 4 + b)
                    for w in range(W):
                        cols = slice(b * SB * W + w, (b + 1) * SB * W, W)
                        link(nc.vector.tensor_copy(c["idx"][:, cols], bank[4 + b % 2][:, w * P:w * P + SB]), False)
                        link(nc.vector.tensor_scalar(c["key"][:, cols], bank[b % 2][:, w * P:w * P + SB],
                                                     c["flag"][:, 0:1], None, ALU.mult), False)
                dve.wait_ge(d, at[0])
                link(nc.vector.tensor_scalar(c["key"][:, :], c["key"][:, :], c["flag"][:, 1:2], None, ALU.subtract), False)
                dve.wait_ge(bias_row_in, 16 * len(BIAS_AT))
                nc.vector.tensor_copy(bpart[:, 0, :], brow[:, :]).then_inc(bias_split, 1)
                dve.wait_ge(bias_split, 1)
                nc.vector.tensor_tensor(bres[:, 0, :], brow[:, :], bpart[:, 0, :], ALU.subtract).then_inc(bias_split, 1)
                dve.wait_ge(bias_split, 2)
                nc.vector.tensor_copy(bpart[:, 1, :], bres[:, 0, :]).then_inc(bias_split, 1)
                dve.wait_ge(bias_split, 3)
                nc.vector.tensor_tensor(bres[:, 1, :], bres[:, 0, :], bpart[:, 1, :], ALU.subtract).then_inc(bias_split, 1)
                dve.wait_ge(bias_split, 4)
                nc.vector.tensor_copy(bpart[:, 2, :], bres[:, 1, :]).then_inc(bias_split, 1)
                dve.wait_ge(w_split, 1)
                nc.vector.tensor_tensor(c["w_lo"][:, :], w_all[:, :], f32(c["w_hi"][:, :]), ALU.subtract).then_inc(w_split, 1)
                dve.wait_ge(a, 1)
                link(nc.vector.reciprocal(rs0[:, :], sqdeg[:, :]))
                link(nc.vector.tensor_tensor(sqdeg[:, :], deg[:, :], rs0[:, :], ALU.mult))
                link(nc.vector.scalar_tensor_tensor(out=counts[:, :], in0=sqdeg[:, :], scalar=-0.5, in1=rs0[:, :],
                                                    op0=ALU.mult, op1=ALU.mult))
                link(nc.vector.scalar_tensor_tensor(out=c["rsdeg"][:, :], in0=counts[:, :], scalar=1.5, in1=rs0[:, :],
                                                    op0=ALU.add, op1=ALU.mult))


def general_pass(nc, sh, c, tables, tag, rows, total, F, normed):
    edges = tables["edges"]
    ER = sh.ER
    with ExitStack() as ctx:
        sb = lambda name, shape, dt=F32: ctx.enter_context(nc.sbuf_tensor(f"{tag}_{name}", shape, dt))
        sem = lambda name: ctx.enter_context(nc.semaphore(f"{tag}_{name}"))
        part = sb("part", [P, T, F])
        parted = sb("parted", [P, T, F])
        st = sb("st", [P, T, 6])
        small = sb("small", [P, 8, T])
        src_i = sb("src_i", [P, 1], I32)
        dst_i = sb("dst_i", [P, 1], I32)
        to_i = sb("to_i", [P, 1], I32)
        row_i = sb("row_i", [P, P], I32)
        dst_f = sb("dst_f", [P, 1])
        row_f = sb("row_f", [P, P])
        same = sb("same", [P, P])
        before = sb("before", [P, P])
        below = sb("below", [P, P])
        spare = sb("spare", [P, 1])
        vec = sb("vec", [P, 6])
        got = sb("got", [P, F])
        msg = sb("msg", [P, F])
        old = sb("old", [P, F])
        new = sb("new", [P, F])
        zero = sb("zero", [P, F])
        sums = ctx.enter_context(nc.psum_tensor(f"{tag}_sums", [P, F], F32))
        made, copied_in, copied_out = sem("made"), sem("copied_in"), sem("copied_out")
        listed, gathered, fetched, placed = sem("listed"), sem("gathered"), sem("fetched"), sem("placed")
        d, a, summed = sem("dve"), sem("act"), sem("summed")
        with nc.Block() as block:
            def stats(dve, wait, rows_in, n, sqrt_at):
                for t in range(n):
                    nc.vector.bn_stats(st[:, t, :], rows_in(t)).then_inc(d, 1)
                wait(n)
                nc.vector.tensor_tensor(small[:, 0, 0:n], st[:, 0:n, 1], st[:, 0:n, 4], ALU.add).then_inc(d, 1)
                nc.vector.tensor_tensor(small[:, 1, 0:n], st[:, 0:n, 1], st[:, 0:n, 4], ALU.subtract).then_inc(d, 1)
                nc.vector.tensor_tensor(small[:, 2, 0:n], st[:, 0:n, 2], st[:, 0:n, 5], ALU.add).then_inc(d, 1)
                wait(n + 3)
                nc.vector.scalar_tensor_tensor(out=small[:, 3, 0:n], in0=small[:, 1, 0:n], scalar=0.25,
                                               in1=small[:, 1, 0:n], op0=ALU.mult, op1=ALU.mult).then_inc(d, 1)
                wait(n + 4)
                nc.vector.scalar_tensor_tensor(out=small[:, 4, 0:n], in0=small[:, 2, 0:n], scalar=1.0 / D,
                                               in1=small[:, 3, 0:n], op0=ALU.mult, op1=ALU.add).then_inc(d, 1)
                dve.wait_ge(a, sqrt_at)
                nc.vector.reciprocal(small[:, 5, 0:n], small[:, 7, 0:n]).then_inc(d, 1)
                wait(n + 6)
                nc.vector.tensor_scalar(small[:, 6, 0:n], small[:, 0, 0:n], 0.5, None, ALU.mult).then_inc(d, 1)
                wait(n + 7)

            NS = T + 7 + T + 1
            NE = (1 + 7 + 2 if normed else 0) + 10
            BASE = sh.S * NS if normed else 0

            @block.gpsimd
            def _(pool):
                flag = pool.value_load(c["flag_int"][0:1, 0:1], min_val=0, max_val=1)
                with pool.If(flag > 0):
                    pool.memset(below[:, :], 0.0).then_inc(made, 1)
                    pool.wait_ge(made, 1)
                    pool.affine_select(out=below[:, :], in_=below[:, :], compare_op=ALU.is_ge, fill=1.0, base=0,
                                       pattern=[[1, P]], channel_multiplier=-1).then_inc(made, 1)
                    pool.memset(zero[:, :], 0.0).then_inc(made, 1)
                    pool.iota(spare[:, :], pattern=[[0, 1]], base=sh.NP, channel_multiplier=1,
                              allow_small_or_imprecise_dtypes=True).then_inc(made, 1)
                    with pool.Fori(0, ER) as i:
                        hold(pool, listed, i * 48 + 48, c["pool_passed"])
                        pool.indirect_dma_start(got[:, :], None, rows,
                                                bass.IndirectOffsetOnAxis(ap=src_i[:, :], axis=0)).then_inc(gathered, 16)
                        hold(pool, d, i * NE + (BASE + NE - 1), c["pool_passed"])
                        pool.indirect_dma_start(old[:, :], None, total,
                                                bass.IndirectOffsetOnAxis(ap=to_i[:, :], axis=0)).then_inc(fetched, 16)
                        hold(pool, d, i * NE + (BASE + NE), c["pool_passed"])
                        pool.indirect_dma_start(total, bass.IndirectOffsetOnAxis(ap=to_i[:, :], axis=0),
                                                new[:, :], None).then_inc(placed, 16)
                        hold(pool, placed, i * 16 + 16, c["pool_passed"])
                with pool.Else():
                    pool.nop()
                pool.nop()

            @block.sync
            def _(sp):
                flag = sp.value_load(c["flag_int"][0:1, 0:1], min_val=0, max_val=1)
                with sp.If(flag > 0):
                    sp.wait_ge(made, 3)
                    sp.dma_start(total[sh.NP:sh.NP + P, :], zero[:, :]).then_inc(copied_out, 16)
                    sp.wait_ge(copied_out, 16)

                    def rows_step(i, frm, to):
                        sp.dma_start(to, frm).then_inc(copied_in, 16)
                        if normed:
                            hold(sp, d, i * NS + NS, c["sp_passed"])
                            sp.dma_start(node_rows(total, i, F), flat(parted[:, :, :])).then_inc(copied_out, 16)
                        else:
                            hold(sp, copied_in, i * 16 + 16, c["sp_passed"])
                            sp.dma_start(node_rows(total, i, F), flat(part[:, :, :])).then_inc(copied_out, 16)
                        hold(sp, copied_out, i * 16 + 32, c["sp_passed"])
                    with sp.Fori(0, sh.S - 1) as i:
                        rows_step(i, node_rows(rows, i, F), flat(part[:, :, :]))
                    if normed:
                        rows_step(sh.S - 1, rows[(sh.S - 1) * R:sh.N, :].rearrange("(p t) f -> p (t f)", t=T),
                                  flat(part[0:sh.LAST, :, :]))
                    else:
                        rows_step(sh.S - 1, node_rows(rows, sh.S - 1, F), flat(part[:, :, :]))
                    with sp.Fori(0, ER) as i:
                        with nc.allow_non_contiguous_dma(reason="one edge on a partition"):
                            sp.dma_start(src_i[:, :], edges[ds(i, 1), 0:P].rearrange("r e -> e r")).then_inc(listed, 16)
                            sp.dma_start(dst_i[:, :], edges[ds(i, 1), P:2 * P].rearrange("r e -> e r")).then_inc(listed, 16)
                        sp.dma_start(row_i[:, :], edges[ds(i, 1), P:2 * P].to_broadcast([P, P])).then_inc(listed, 16)
                        hold(sp, placed, i * 16 + 16, c["sp_passed"])
                with sp.Else():
                    sp.nop()
                sp.nop()

            @block.scalar
            def _(act):
                flag = act.value_load(c["flag_int"][0:1, 0:1], min_val=0, max_val=1)
                with act.If(flag > 0):
                    if normed:
                        with act.Fori(0, sh.S) as i:
                            act.wait_ge(d, i * NS + (T + 5))
                            nc.scalar.activation(small[:, 7, 0:T], small[:, 4, 0:T], ACT.Sqrt, bias=c["eps"][:, :]).then_inc(a, 1)
                            act.wait_ge(a, i + 1)
                        with act.Fori(0, ER) as i:
                            act.wait_ge(d, i * NE + (BASE + 6))
                            nc.scalar.activation(small[:, 7, 0:1], small[:, 4, 0:1], ACT.Sqrt, bias=c["eps"][:, :]).then_inc(a, 1)
                            act.wait_ge(a, i + (sh.S + 1))
                    else:
                        act.nop()
                with act.Else():
                    act.nop()
                act.nop()

            @block.tensor
            def _(pe):
                flag = pe.value_load(c["flag_int"][0:1, 0:1], min_val=0, max_val=1)
                with pe.If(flag > 0):
                    with pe.Fori(0, ER) as i:
                        pe.wait_ge(d, i * NE + (BASE + NE - 1))
                        if not normed:
                            pe.wait_ge(gathered, i * 16 + 16)
                        nc.tensor.matmul(sums[:, :], same[:, :], (msg if normed else got)[:, :],
                                         start=True, stop=True).then_inc(summed, 1)
                with pe.Else():
                    pe.nop()
                pe.nop()

            @block.vector
            def _(dve):
                flag = dve.value_load(c["flag_int"][0:1, 0:1], min_val=0, max_val=1)
                with dve.If(flag > 0):
                    if normed:
                        with dve.Fori(0, sh.S) as i:
                            dve.wait_ge(copied_in, i * 16 + 16)
                            wait = lambda k: dve.wait_ge(d, i * NS + k)
                            stats(dve, wait, lambda t: part[:, t, :], T, i + 1)
                            for t in range(T):
                                nc.vector.tensor_scalar(part[:, t, :], part[:, t, :], small[:, 6, t:t + 1],
                                                        small[:, 5, t:t + 1], ALU.subtract, ALU.mult).then_inc(d, 1)
                            wait(T + 7 + T)
                            dve.wait_ge(copied_out, i * 16 + 16)
                            nc.vector.tensor_scalar(parted[:, :, :], part[:, :, :], 0.0, None, ALU.max).then_inc(d, 1)
                            wait(NS)
                    dve.wait_ge(made, 4)
                    with dve.Fori(0, ER) as i:
                        wait = lambda k: dve.wait_ge(d, i * NE + (BASE + k))
                        k0 = 0
                        if normed:
                            dve.wait_ge(gathered, i * 16 + 16)
                            stats(dve, wait, lambda t: got[:, :], 1, i + (sh.S + 1))
                            nc.vector.tensor_scalar(got[:, :], got[:, :], small[:, 6, 0:1],
                                                    small[:, 5, 0:1], ALU.subtract, ALU.mult).then_inc(d, 1)
                            wait(9)
                            nc.vector.tensor_scalar(msg[:, :], got[:, :], 0.0, None, ALU.max).then_inc(d, 1)
                            k0 = 10
                        dve.wait_ge(listed, i * 48 + 48)
                        nc.vector.tensor_copy(dst_f[:, :], dst_i[:, :]).then_inc(d, 1)
                        nc.vector.tensor_copy(row_f[:, :], row_i[:, :]).then_inc(d, 1)
                        wait(k0 + 2)
                        nc.vector.tensor_scalar(same[:, :], row_f[:, :], dst_f[:, 0:1], None, ALU.is_equal).then_inc(d, 1)
                        nc.vector.tensor_tensor(vec[:, 3:4], dst_f[:, :], spare[:, :], ALU.subtract).then_inc(d, 1)
                        wait(k0 + 4)
                        nc.vector.tensor_tensor(before[:, :], same[:, :], below[:, :], ALU.mult).then_inc(d, 1)
                        wait(k0 + 5)
                        nc.vector.reduce_sum(vec[:, 0:1], before[:, :], axis=AXX).then_inc(d, 1)
                        wait(k0 + 6)
                        nc.vector.tensor_scalar(vec[:, 1:2], vec[:, 0:1], 0.0, vec[:, 3:4], ALU.is_equal, ALU.mult).then_inc(d, 1)
                        nc.vector.tensor_scalar(vec[:, 2:3], dst_f[:, :], float(FAR), None, ALU.is_lt).then_inc(d, 1)
                        wait(k0 + 8)
                        nc.vector.scalar_tensor_tensor(out=to_i[:, :], in0=vec[:, 1:2], scalar=vec[:, 2:3],
                                                       in1=spare[:, :], op0=ALU.mult, op1=ALU.add).then_inc(d, 1)
                        dve.wait_ge(fetched, i * 16 + 16)
                        dve.wait_ge(summed, i + 1)
                        nc.vector.tensor_tensor(new[:, :], sums[:, :], old[:, :], ALU.add).then_inc(d, 1)
                        wait(k0 + 10)
                        dve.wait_ge(placed, i * 16 + 16)
                with dve.Else():
                    dve.nop()
                dve.nop()


def load_own(sp, sh, c, plain, total, body):
    flag = sp.value_load(c["flag_int"][0:1, 0:1], min_val=0, max_val=1)
    with sp.If(flag > 0):
        body(total)
        sp.nop()
    with sp.Else():
        body(plain)
        sp.nop()
    sp.nop()




def gin_first(nc, sh, c, tables, x):
    S = sh.S
    live = lambda s: not isinstance(s, int) or 0 <= s < S
    h1 = tables["h1"]
    with ExitStack() as ctx:
        sb = lambda name, shape, dt=F32: ctx.enter_context(nc.sbuf_tensor(f"a_{name}", shape, dt))
        ps = lambda name: ctx.enter_context(nc.psum_tensor(f"a_{name}", [P, 512], F32))
        sem = lambda name: ctx.enter_context(nc.semaphore(f"a_{name}"))
        TW = T + W
        xg = sb("xg", [P, 2, TW, D])
        ix = sb("ix", [P, 2, W], I32)
        st = sb("st", [P, 2, TW, 6])
        msum, mdif, vsum, msq, var, dev, rstd, mean, nmr = (
            sb(n, [P, 2, TW]) for n in ("msum", "mdif", "vsum", "msq", "var", "dev", "rstd", "mean", "nmr"))
        xn = sb("xn", [P, 2, T, D])
        gc = sb("gc", [P, 2, W, D])
        hot = sb("hot", [P, 2, W, T, WP[0]])
        ht_hi, ht_lo = sb("ht_hi", [P, 2, R], F32R), sb("ht_lo", [P, 2, R], F32R)
        at_hi, at_lo = sb("at_hi", [P, 2, 2, R], F32R), sb("at_lo", [P, 2, 2, R], F32R)
        hout = sb("hout", [P, 2, T, DH])
        psT = [ps("psT0"), ps("psT1")]
        psA = [ps("psA0"), ps("psA1")]
        psB = [ps(f"psB{i}") for i in range(2)]
        own_loaded = [sem("own_loaded0"), sem("own_loaded1")]
        gath_loaded = [sem("gath_loaded0"), sem("gath_loaded1")]
        stored = [sem("stored0"), sem("stored1")]
        ix_ready, var_ready, dev_ready, rstd_ready = sem("ix_ready"), sem("var_ready"), sem("dev_ready"), sem("rstd_ready")
        own_normed, gath_ready, small_done = sem("own_normed"), sem("gath_ready"), sem("small_done")
        t_done, t_hi, t_lo, a_done, a_hi, a_lo = (sem("t_done"), sem("t_hi"), sem("t_lo"), sem("a_done"), sem("a_hi"),
                                                  sem("a_lo"))
        b_done, b_read = sem("b_done"), sem("b_read")

        with nc.Block() as block:
            @block.sync
            def _(sp):
                def body(table):
                    def step(s, p):
                        q = 1 - p
                        if live(s + 3):
                            if live(s + 1):
                                hold(sp, own_normed, s + 2, c["sp_passed"])
                                hold(sp, gath_ready, s + 2, c["sp_passed"])
                            if isinstance(s, int) and s + 3 == S - 1:
                                rows = table[(S - 1) * R:sh.N, :].rearrange("(p t) f -> p (t f)", t=T)
                                to = flat(xg[0:sh.LAST, q, 0:T, :])
                            else:
                                rows, to = node_rows(table, s + 3, D), flat(xg[:, q, 0:T, :])
                            sp.dma_start(to, rows).then_inc(own_loaded[q], 16)
                        if live(s - 1):
                            hold(sp, b_read, s * 2, c["sp_passed"])
                            sp.dma_start(node_rows(h1, s - 1, DH), flat(hout[:, q, :, :])).then_inc(stored[q], 16)
                    run_pipeline(sp, sh, step, -3, S)
                load_own(sp, sh, c, x, tables["sum128"], body)
                sp.wait_ge(stored[0], 8 * S)
                sp.wait_ge(stored[1], 8 * S)

            @block.gpsimd
            def _(pool):
                def step(s, p):
                    q = 1 - p
                    if live(s + 3):
                        if live(s + 1):
                            hold(pool, gath_ready, s + 2, c["pool_passed"])
                        pool.tensor_copy(ix[:, q, :], c["idx"][:, ds((s + 3) * W, W)]).then_inc(ix_ready, 1)
                        hold(pool, ix_ready, s + 4, c["pool_passed"])
                        for w in range(W):
                            pool.indirect_dma_start(xg[:, q, T + w, :], None, x,
                                                    bass.IndirectOffsetOnAxis(ap=ix[:, q, w:w + 1], axis=0)
                                                    ).then_inc(gath_loaded[q], 16)
                run_pipeline(pool, sh, step, -3, S)

            @block.vector
            def _(dve):
                def step(s, p):
                    q = 1 - p
                    if live(s + 2):
                        n = s + 2
                        dve.wait_ge(own_loaded[p], count_of(n, p))
                        dve.wait_ge(gath_loaded[p], count_of(n, p) * W)
                        for t in range(TW):
                            nc.vector.bn_stats(st[:, p, t, :], xg[:, p, t, :]).then_inc(small_done, 1)
                        dve.wait_ge(small_done, n * 15 + 7)
                        nc.vector.tensor_tensor(msum[:, p, :], st[:, p, :, 1], st[:, p, :, 4], ALU.add).then_inc(small_done, 1)
                        nc.vector.tensor_tensor(mdif[:, p, :], st[:, p, :, 1], st[:, p, :, 4], ALU.subtract).then_inc(small_done, 1)
                        nc.vector.tensor_tensor(vsum[:, p, :], st[:, p, :, 2], st[:, p, :, 5], ALU.add).then_inc(small_done, 1)
                        dve.wait_ge(small_done, n * 15 + 9)
                        nc.vector.scalar_tensor_tensor(out=msq[:, p, :], in0=mdif[:, p, :], scalar=0.25, in1=mdif[:, p, :],
                                                       op0=ALU.mult, op1=ALU.mult).then_inc(small_done, 1)
                        dve.wait_ge(small_done, n * 15 + 11)
                        nc.vector.scalar_tensor_tensor(out=var[:, p, :], in0=vsum[:, p, :], scalar=1.0 / D, in1=msq[:, p, :],
                                                       op0=ALU.mult, op1=ALU.add).then_inc(var_ready, 1)
                        nc.vector.tensor_scalar(mean[:, p, :], msum[:, p, :], 0.5, None, ALU.mult).then_inc(small_done, 1)
                    if live(s):
                        for m in range(2):
                            dve.wait_ge(a_hi, s * 2 + (m + 1))
                            nc.vector.scalar_tensor_tensor(out=at_lo[:, p, m, :], in0=psA[m][:, :], scalar=0.0,
                                                           in1=f32(at_hi[:, p, m, :]), op0=ALU.max,
                                                           op1=ALU.subtract).then_inc(a_lo, 1)
                    if live(s + 1):
                        dve.wait_ge(t_hi, s + 2)
                        nc.vector.tensor_tensor(ht_lo[:, q, :], psT[q][:, :], f32(ht_hi[:, q, :]), ALU.subtract).then_inc(t_lo, 1)
                    if live(s + 2):
                        n = s + 2
                        dve.wait_ge(dev_ready, n + 1)
                        nc.vector.reciprocal(rstd[:, p, :], dev[:, p, :]).then_inc(small_done, 1)
                        dve.wait_ge(small_done, n * 15 + 13)
                        nc.vector.scalar_tensor_tensor(out=nmr[:, p, 0:T], in0=mean[:, p, 0:T], scalar=-1.0, in1=rstd[:, p, 0:T],
                                                       op0=ALU.mult, op1=ALU.mult).then_inc(small_done, 1)
                        dve.wait_ge(small_done, n * 15 + 14)
                        nc.vector.tensor_scalar(nmr[:, p, 0:T], nmr[:, p, 0:T], c["flag"][:, 0:1], None,
                                                ALU.mult).then_inc(rstd_ready, 1)
                        nc.vector.tensor_scalar(rstd[:, p, 0:T], rstd[:, p, 0:T], c["flag"][:, 0:1], c["flag"][:, 1:2],
                                                ALU.mult, ALU.add).then_inc(rstd_ready, 1)
                        if live(n - 2):
                            dve.wait_ge(t_done, s + 1)
                        for w in range(W):
                            nc.vector.tensor_scalar(gc[:, p, w, :], xg[:, p, T + w, :], mean[:, p, T + w:T + w + 1], 0.0,
                                                    ALU.subtract, ALU.max)
                        for w in range(W):
                            ins = nc.vector.tensor_scalar(hot[:, p, w, :, 0:WP[w]], c["iota"][:, :, 0:WP[w]],
                                                          c["key"][:, ds(n * W + w, 1)], rstd[:, p, T + w:T + w + 1],
                                                          ALU.is_equal, ALU.mult)
                        ins.then_inc(gath_ready, 1)
                        nc.vector.tensor_scalar(msq[:, p, :], mean[:, p, :], 1.0, None, ALU.mult).then_inc(small_done, 1)
                run_pipeline(dve, sh, step, -2, S)

            @block.scalar
            def _(act):
                def step(s, p):
                    q = 1 - p
                    if live(s):
                        for m in range(2):
                            act.wait_ge(a_done, s * 2 + (m + 1))
                            if live(s - 2) and m == 0:
                                act.wait_ge(b_done, (s - 1) * 2)
                            nc.scalar.activation(at_hi[:, p, m, :], psA[m][:, :], ACT.Relu).then_inc(a_hi, 1)
                    if live(s + 2):
                        act.wait_ge(var_ready, s + 3)
                        nc.scalar.activation(dev[:, p, :], var[:, p, :], ACT.Sqrt, bias=c["eps"][:, :]).then_inc(dev_ready, 1)
                    if live(s + 1):
                        act.wait_ge(t_done, s + 2)
                        nc.scalar.activation(ht_hi[:, q, :], psT[q][:, :], ACT.Copy).then_inc(t_hi, 1)
                    if live(s + 2):
                        act.wait_ge(rstd_ready, (s + 3) * 2)
                        if live(s):
                            act.wait_ge(t_done, s + 1)
                        for t in range(T):
                            ins = nc.scalar.activation(xn[:, p, t, :], xg[:, p, t, :], ACT.Relu,
                                                       bias=nmr[:, p, t:t + 1], scale=rstd[:, p, t:t + 1])
                        ins.then_inc(own_normed, 1)
                    if live(s - 1):
                        if live(s - 3):
                            act.wait_ge(stored[q], count_of(s - 3, q))
                        for half in range(2):
                            act.wait_ge(b_done, s * 2 - (1 - half))
                            nc.scalar.activation(flat(hout[:, q, 2 * half:2 * half + 2, :]), psB[half][:, :],
                                                 ACT.Relu).then_inc(b_read, 1)
                run_pipeline(act, sh, step, -2, S)

            @block.tensor
            def _(pe):
                def step(s, p):
                    q = 1 - p
                    if live(s):
                        pe.wait_ge(t_lo, s + 1)
                        for m in range(2):
                            if live(s - 1):
                                pe.wait_ge(a_lo, (s - 1) * 2 + (m + 1))
                            nc.tensor.matmul(psA[m][:, :], bias_parts(c, "b1a", m * P, (m + 1) * P), c["ones3"][:, :],
                                             start=True, stop=False)
                            product(nc, psA[m][:, :], *weight(c, "w1a", 0, m * P, (m + 1) * P), ht_hi[:, p, :],
                                    ht_lo[:, p, :], False, True).then_inc(a_done, 1)
                    if live(s + 1):
                        pe.wait_ge(own_normed, s + 2)
                        pe.wait_ge(gath_ready, s + 2)
                        if live(s - 1):
                            pe.wait_ge(t_lo, s)
                        for t in range(T):
                            nc.tensor.matmul(psT[q][:, t * P:(t + 1) * P], xn[:, q, t, :], c["ident"][:, :],
                                             is_transpose=True, start=t == 0, stop=False)
                        for w in range(W):
                            ins = nc.tensor.matmul(windows(psT[q][:, :])[:, :, W0[w]:W0[w] + WP[w]], gc[:, q, w, :],
                                                   hot[:, q, w, :, 0:WP[w]], start=False, stop=w == W - 1)
                        ins.then_inc(t_done, 1)
                    if live(s - 1):
                        pe.wait_ge(a_lo, s * 2)
                        for t in range(T):
                            if live(s - 2) and t % 2 == 0:
                                pe.wait_ge(b_read, (s - 2) * 2 + (t // 2 + 1))
                            acc = psB[t // 2][:, (t % 2) * DH:(t % 2 + 1) * DH]
                            nc.tensor.matmul(acc, c["ones3"][:, 0:P], bias_parts(c, "b1b", 0, DH), start=t % 2 == 0, stop=False)
                            for k in range(2):
                                rows = at_hi[:, q, k, t * P:(t + 1) * P], at_lo[:, q, k, t * P:(t + 1) * P]
                                ins = product(nc, acc, *rows, *weight(c, "w1b", k), False, t % 2 == 1 and k == 1)
                            if t % 2 == 1:
                                ins.then_inc(b_done, 1)
                run_pipeline(pe, sh, step, -1, S)


def gin_second(nc, sh, c, tables, x):
    S = sh.S
    live = lambda s: not isinstance(s, int) or 0 <= s < S
    h1, x1, g1 = tables["h1"], tables["x1"], tables["g1"]
    with ExitStack() as ctx:
        sb = lambda name, shape, dt=F32: ctx.enter_context(nc.sbuf_tensor(f"b_{name}", shape, dt))
        ps = lambda name: ctx.enter_context(nc.psum_tensor(f"b_{name}", [P, 512], F32))
        sem = lambda name: ctx.enter_context(nc.semaphore(f"b_{name}"))
        own = sb("own", [P, 2, T, DH])
        gat = sb("gat", [P, 2, W, DH])
        gat_hi, gat_lo = sb("gat_hi", [P, 2, W, DH], F32R), sb("gat_lo", [P, 2, W, DH], F32R)
        ix = sb("ix", [P, 2, W], I32)
        hot = sb("hot", [P, 2, W, T, WP[0]], F32R)
        ht_hi, ht_lo = sb("ht_hi", [P, 2, 2, R], F32R), sb("ht_lo", [P, 2, 2, R], F32R)
        at_hi, at_lo = sb("at_hi", [P, 2, 2, R], F32R), sb("at_lo", [P, 2, 2, R], F32R)
        bt = sb("bt", [P, 2, R])
        xr = sb("xr", [P, 2, T, D])
        xs = sb("xs", [P, 2, T, D])
        hn = sb("hn", [P, 2, T, D])
        st = sb("st", [P, 2, T, 6])
        msum, mdif, vsum, msq, var, dev, rstd, scale, shift = (
            sb(n, [P, 2, T]) for n in ("msum", "mdif", "vsum", "msq", "var", "dev", "rstd", "scale", "shift"))
        psT = [ps("psT0"), ps("psT1")]
        psA = [ps("psA0"), ps("psA1")]
        psC, psB = ps("psC"), ps("psB")
        own_loaded = [sem("own_loaded0"), sem("own_loaded1")]
        gath_loaded = [sem("gath_loaded0"), sem("gath_loaded1")]
        x_loaded = [sem("x_loaded0"), sem("x_loaded1")]
        x_stored = [sem("x_stored0"), sem("x_stored1")]
        g_stored = [sem("g_stored0"), sem("g_stored1")]
        ix_ready, hot_ready, small_done = sem("ix_ready"), sem("hot_ready"), sem("small_done")
        x_ready, var_ready, dev_ready, scale_ready, normed = (sem("x_ready"), sem("var_ready"), sem("dev_ready"),
                                                              sem("scale_ready"), sem("normed"))
        c_done, bt_ready = sem("c_done"), sem("bt_ready")
        t_done, t_hi, t_lo, a_done, a_hi, a_lo = (sem("t_done"), sem("t_hi"), sem("t_lo"), sem("a_done"), sem("a_hi"),
                                                  sem("a_lo"))
        b_done, gath_hi, gath_lo = sem("b_done"), sem("gath_hi"), sem("gath_lo")

        with nc.Block() as block:
            @block.sync
            def _(sp):
                def body(table):
                    def step(s, p):
                        q = 1 - p
                        if live(s + 3):
                            if live(s + 1):
                                hold(sp, t_done, (s + 2) * 2, c["sp_passed"])
                            sp.dma_start(flat(own[:, q, :, :]), node_rows(table, s + 3, DH)).then_inc(own_loaded[q], 16)
                        if live(s - 2):
                            hold(sp, x_ready, s - 1, c["sp_passed"])
                            sp.dma_start(node_rows(x1, s - 2, D), flat(xs[:, p, :, :])).then_inc(x_stored[p], 16)
                        if live(s):
                            if isinstance(s, int) and s == S - 1:
                                rows = x[(S - 1) * R:sh.N, :].rearrange("(p t) f -> p (t f)", t=T)
                                to = flat(xr[0:sh.LAST, p, :, :])
                            else:
                                rows, to = node_rows(x, s, D), flat(xr[:, p, :, :])
                            sp.dma_start(to, rows).then_inc(x_loaded[p], 16)
                        if live(s - 3):
                            hold(sp, normed, s - 2, c["sp_passed"])
                            sp.dma_start(node_rows(g1, s - 3, D), flat(hn[:, q, :, :])).then_inc(g_stored[q], 16)
                    run_pipeline(sp, sh, step, -3, S + 2)
                load_own(sp, sh, c, h1, tables["sum256"], body)
                for done in x_stored + g_stored:
                    sp.wait_ge(done, 8 * S)

            @block.gpsimd
            def _(pool):
                def step(s, p):
                    q = 1 - p
                    if live(s + 3):
                        if live(s + 1):
                            hold(pool, gath_lo, s + 2, c["pool_passed"])
                        pool.tensor_copy(ix[:, q, :], c["idx"][:, ds((s + 3) * W, W)]).then_inc(ix_ready, 1)
                        hold(pool, ix_ready, s + 4, c["pool_passed"])
                        for w in range(W):
                            pool.indirect_dma_start(gat[:, q, w, :], None, h1,
                                                    bass.IndirectOffsetOnAxis(ap=ix[:, q, w:w + 1], axis=0)
                                                    ).then_inc(gath_loaded[q], 16)
                    if live(s + 2):
                        hold(pool, gath_hi, s + 3, c["pool_passed"])
                        if live(s):
                            hold(pool, t_done, (s + 1) * 2, c["pool_passed"])
                        pool.tensor_tensor(gat_lo[:, p, :, :], gat[:, p, :, :], f32(gat_hi[:, p, :, :]),
                                           ALU.subtract).then_inc(gath_lo, 1)
                run_pipeline(pool, sh, step, -3, S)

            @block.vector
            def _(dve):
                def step(s, p):
                    q = 1 - p

                    def one_hot(w):
                        if live(s + 2):
                            if live(s) and w == 0:
                                dve.wait_ge(t_done, (s + 1) * 2)
                            nc.vector.tensor_scalar(hot[:, p, w, :, 0:WP[w]], c["iota"][:, :, 0:WP[w]],
                                                    c["key"][:, ds((s + 2) * W + w, 1)], None,
                                                    ALU.is_equal).then_inc(hot_ready, 1)
                    if live(s - 3):
                        n = s - 3
                        for t in range(T):
                            nc.vector.bn_stats(st[:, q, t, :], xs[:, q, t, :]).then_inc(small_done, 1)
                        dve.wait_ge(small_done, n * 10 + 4)
                        nc.vector.tensor_tensor(mdif[:, q, :], st[:, q, :, 1], st[:, q, :, 4], ALU.subtract).then_inc(small_done, 1)
                        nc.vector.tensor_tensor(vsum[:, q, :], st[:, q, :, 2], st[:, q, :, 5], ALU.add).then_inc(small_done, 1)
                        nc.vector.tensor_tensor(msum[:, q, :], st[:, q, :, 1], st[:, q, :, 4], ALU.add).then_inc(small_done, 1)
                        dve.wait_ge(small_done, n * 10 + 5)
                        nc.vector.scalar_tensor_tensor(out=msq[:, q, :], in0=mdif[:, q, :], scalar=0.25, in1=mdif[:, q, :],
                                                       op0=ALU.mult, op1=ALU.mult).then_inc(small_done, 1)
                        dve.wait_ge(small_done, n * 10 + 8)
                        nc.vector.scalar_tensor_tensor(out=var[:, q, :], in0=vsum[:, q, :], scalar=1.0 / D, in1=msq[:, q, :],
                                                       op0=ALU.mult, op1=ALU.add).then_inc(var_ready, 1)
                    one_hot(0)
                    if live(s - 3):
                        dve.wait_ge(dev_ready, n + 1)
                        nc.vector.reciprocal(rstd[:, q, :], dev[:, q, :]).then_inc(small_done, 1)
                        dve.wait_ge(small_done, n * 10 + 9)
                        nc.vector.tensor_tensor(scale[:, q, :], rstd[:, q, :], c["rsdeg"][:, ds(n * T, T)],
                                                ALU.mult).then_inc(small_done, 1)
                        dve.wait_ge(small_done, n * 10 + 10)
                        nc.vector.scalar_tensor_tensor(out=shift[:, q, :], in0=msum[:, q, :], scalar=-0.5, in1=scale[:, q, :],
                                                       op0=ALU.mult, op1=ALU.mult).then_inc(scale_ready, 1)
                    one_hot(1)
                    if live(s):
                        for m in range(2):
                            dve.wait_ge(a_hi, s * 2 + (m + 1))
                            nc.vector.scalar_tensor_tensor(out=at_lo[:, p, m, :], in0=psA[m][:, :], scalar=0.0,
                                                           in1=f32(at_hi[:, p, m, :]), op0=ALU.max,
                                                           op1=ALU.subtract).then_inc(a_lo, 1)
                    one_hot(2)
                    if live(s + 1):
                        for k in range(2):
                            dve.wait_ge(t_hi, (s + 1) * 2 + (k + 1))
                            nc.vector.tensor_tensor(ht_lo[:, q, k, :], psT[k][:, :], f32(ht_hi[:, q, k, :]),
                                                    ALU.subtract).then_inc(t_lo, 1)
                    if live(s - 2):
                        dve.wait_ge(b_done, s - 1)
                        dve.wait_ge(x_loaded[p], count_of(s - 2, p))
                        if live(s - 4):
                            dve.wait_ge(x_stored[p], count_of(s - 4, p))
                            dve.wait_ge(normed, s - 3)
                        nc.vector.tensor_tensor(flat(xs[:, p, :, :]), psB[:, :], flat(xr[:, p, :, :]), ALU.add).then_inc(x_ready, 1)
                        dve.wait_ge(x_ready, s - 1)
                run_pipeline(dve, sh, step, -2, S + 2)

            @block.scalar
            def _(act):
                def step(s, p):
                    q = 1 - p
                    if live(s - 2):
                        act.wait_ge(c_done, s - 1)
                        if live(s - 4):
                            act.wait_ge(b_done, s - 3)
                        nc.scalar.activation(bt[:, p, :], psC[:, :], ACT.Identity, bias=c["b2b"][:, :]).then_inc(bt_ready, 1)
                    if live(s + 2):
                        act.wait_ge(gath_loaded[p], count_of(s + 2, p) * W)
                        if live(s):
                            act.wait_ge(t_done, (s + 1) * 2)
                        nc.scalar.activation(gat_hi[:, p, :, :], gat[:, p, :, :], ACT.Copy).then_inc(gath_hi, 1)
                    if live(s - 3):
                        act.wait_ge(var_ready, s - 2)
                        nc.scalar.activation(dev[:, q, :], var[:, q, :], ACT.Sqrt, bias=c["eps"][:, :]).then_inc(dev_ready, 1)

                    def hidden_hi(m):
                        act.wait_ge(a_done, s * 2 + (m + 1))
                        if live(s - 2) and m == 0:
                            act.wait_ge(c_done, s - 1)
                        nc.scalar.activation(at_hi[:, p, m, :], psA[m][:, :], ACT.Relu).then_inc(a_hi, 1)

                    def sums_hi(k):
                        act.wait_ge(t_done, (s + 1) * 2 + (k + 1))
                        if live(s - 1) and k == 0:
                            act.wait_ge(a_done, s * 2)
                        nc.scalar.activation(ht_hi[:, q, k, :], psT[k][:, :], ACT.Copy).then_inc(t_hi, 1)

                    def normalise(rows):
                        for t in rows:
                            ins = nc.scalar.activation(hn[:, q, t, :], xs[:, q, t, :], ACT.Relu,
                                                       bias=shift[:, q, t:t + 1], scale=scale[:, q, t:t + 1])
                        return ins
                    if live(s):
                        hidden_hi(0)
                    if live(s):
                        hidden_hi(1)
                    if live(s - 3):
                        act.wait_ge(scale_ready, s - 2)
                        if live(s - 5):
                            act.wait_ge(g_stored[q], count_of(s - 5, q))
                        normalise((0, 1))
                    if live(s + 1):
                        sums_hi(0)
                        sums_hi(1)
                    if live(s - 3):
                        normalise((2, 3)).then_inc(normed, 1)
                run_pipeline(act, sh, step, -2, S + 2)

            @block.tensor
            def _(pe):
                def step(s, p):
                    q = 1 - p
                    if live(s):
                        pe.wait_ge(t_lo, s * 2 + 1)
                        for m in range(2):
                            if live(s - 1):
                                pe.wait_ge(a_lo, (s - 1) * 2 + (m + 1))
                            nc.tensor.matmul(psA[m][:, :], bias_parts(c, "b2a", m * P, (m + 1) * P), c["ones3"][:, :],
                                             start=True, stop=False)
                            for k in range(2):
                                if m == 0 and k == 1:
                                    pe.wait_ge(t_lo, (s + 1) * 2)
                                ins = product(nc, psA[m][:, :], *weight(c, "w2a", k, m * P, (m + 1) * P),
                                              ht_hi[:, p, k, :], ht_lo[:, p, k, :], False, k == 1)
                            ins.then_inc(a_done, 1)
                    if live(s + 1):
                        pe.wait_ge(own_loaded[q], count_of(s + 1, q))
                        pe.wait_ge(gath_lo, s + 2)
                        pe.wait_ge(hot_ready, (s + 2) * W)
                        if live(s):
                            pe.wait_ge(t_lo, (s + 1) * 2)
                        for k in range(2):
                            for t in range(T):
                                nc.tensor.matmul(psT[k][:, t * P:(t + 1) * P], own[:, q, t, k * P:(k + 1) * P],
                                                 c["ident"][:, :], is_transpose=True, start=t == 0, stop=False)
                            for w in range(W):
                                for rows in (gat_lo, gat_hi):
                                    ins = nc.tensor.matmul(windows(psT[k][:, :])[:, :, W0[w]:W0[w] + WP[w]],
                                                           rows[:, q, w, k * P:(k + 1) * P], hot[:, q, w, :, 0:WP[w]],
                                                           start=False, stop=w == W - 1 and rows is gat_hi)
                            ins.then_inc(t_done, 1)
                    if live(s - 2):
                        pe.wait_ge(bt_ready, s - 1)
                        if live(s - 3):
                            pe.wait_ge(x_ready, s - 2)
                        for t in range(T):
                            ins = nc.tensor.matmul(psB[:, t * P:(t + 1) * P], bt[:, p, t * P:(t + 1) * P], c["ident"][:, :],
                                                   is_transpose=True, start=t == 0, stop=t == T - 1)
                        ins.then_inc(b_done, 1)
                    if live(s - 1):
                        pe.wait_ge(a_lo, s * 2)
                        if live(s - 2):
                            pe.wait_ge(bt_ready, s - 1)
                        for k in range(2):
                            ins = product(nc, psC[:, :], *weight(c, "w2b", k), at_hi[:, q, k, :], at_lo[:, q, k, :],
                                          k == 0, k == 1)
                        ins.then_inc(c_done, 1)
                run_pipeline(pe, sh, step, -1, S + 1)


def gcn(nc, sh, c, tables, tag, g, w_name, bias, out, final):
    S = sh.S
    live = lambda s: not isinstance(s, int) or 0 <= s < S
    x1 = tables["x1"]
    with ExitStack() as ctx:
        sb = lambda name, shape, dt=F32: ctx.enter_context(nc.sbuf_tensor(f"{tag}_{name}", shape, dt))
        ps = lambda name: ctx.enter_context(nc.psum_tensor(f"{tag}_{name}", [P, 512], F32))
        sem = lambda name: ctx.enter_context(nc.semaphore(f"{tag}_{name}"))
        K = 4
        own = sb("own", [P, K, T, D])
        gat = sb("gat", [P, K, W, D])
        ix = sb("ix", [P, K, W], I32)
        hot = sb("hot", [P, 2, W, T, WP[0]])
        st_hi, st_lo = sb("st_hi", [P, 2, R], F32R), sb("st_lo", [P, 2, R], F32R)
        v = sb("v", [P, 2, T, D])
        xs = sb("xs", [P, K, T, D]) if final else None
        res = sb("res", [P, K, T, D])
        psT = [ps("psT0"), ps("psT1")]
        psZ = [ps("psZ0"), ps("psZ1")]
        own_loaded = [sem(f"own_loaded{i}") for i in range(K)]
        gath_loaded = [sem(f"gath_loaded{i}") for i in range(K)]
        x_loaded = [sem(f"x_loaded{i}") for i in range(K if final else 0)]
        stored = [sem(f"stored{i}") for i in range(K)]
        ix_ready, hot_ready, t_done, t_hi, t_lo, z_done, v_ready, res_ready = (
            sem("ix_ready"), sem("hot_ready"), sem("t_done"), sem("t_hi"), sem("t_lo"), sem("z_done"), sem("v_ready"),
            sem("res_ready"))

        with nc.Block() as block:
            @block.sync
            def _(sp):
                def body(table):
                    def step(s, p):
                        if live(s + 4):
                            if live(s):
                                hold(sp, t_done, s + 1, c["sp_passed"])
                            sp.dma_start(flat(own[:, p, :, :]), node_rows(table, s + 4, D)).then_inc(own_loaded[p], 16)
                        if live(s - 1):
                            q = (p - 1) % K
                            hold(sp, res_ready, s, c["sp_passed"])
                            if final and isinstance(s, int) and s == S:
                                rows = out[(S - 1) * R:sh.N, :].rearrange("(p t) f -> p (t f)", t=T)
                                frm = flat(res[0:sh.LAST, q, :, :])
                            else:
                                rows, frm = node_rows(out, s - 1, D), flat(res[:, q, :, :])
                            sp.dma_start(rows, frm).then_inc(stored[q], 16)
                        if final and live(s + 3):
                            sp.dma_start(flat(xs[:, (p + 3) % K, :, :]), node_rows(x1, s + 3, D)
                                         ).then_inc(x_loaded[(p + 3) % K], 16)
                    run_pipeline(sp, sh, step, -4, S, K)
                load_own(sp, sh, c, g, tables["sum128"], body)
                for i in range(K):
                    sp.wait_ge(stored[i], 16 * len(range(i, S, K)))

            @block.gpsimd
            def _(pool):
                def step(s, p):
                    if live(s + 4):
                        if live(s):
                            hold(pool, t_done, s + 1, c["pool_passed"])
                        hold(pool, ix_ready, s + 5, c["pool_passed"])
                        for w in range(W):
                            pool.indirect_dma_start(gat[:, p, w, :], None, g,
                                                    bass.IndirectOffsetOnAxis(ap=ix[:, p, w:w + 1], axis=0)
                                                    ).then_inc(gath_loaded[p], 16)
                run_pipeline(pool, sh, step, -4, S, K)

            @block.vector
            def _(dve):
                def step(s, p):
                    r, p, q = p, p % 2, (p + 1) % 2
                    if live(s + 2):
                        if live(s):
                            dve.wait_ge(t_done, s + 1)
                        for w in range(W):
                            ins = nc.vector.tensor_scalar(hot[:, p, w, :, 0:WP[w]], c["iota"][:, :, 0:WP[w]],
                                                          c["key"][:, ds((s + 2) * W + w, 1)], None, ALU.is_equal)
                        ins.then_inc(hot_ready, 1)
                    if live(s + 1):
                        dve.wait_ge(t_hi, s + 2)
                        nc.vector.tensor_tensor(st_lo[:, q, :], psT[q][:, :], f32(st_hi[:, q, :]),
                                                ALU.subtract).then_inc(t_lo, 1)
                    if live(s):
                        dve.wait_ge(z_done, s + 1)
                        if not final and live(s - 2):
                            dve.wait_ge(res_ready, s - 1)
                        for t in range(T):
                            ins = nc.vector.scalar_tensor_tensor(out=v[:, p, t, :], in0=psZ[p][:, t * D:(t + 1) * D],
                                                                 scalar=c["rsdeg"][:, ds(s * T + t, 1)],
                                                                 in1=bias[:, :], op0=ALU.mult, op1=ALU.add)
                        ins.then_inc(v_ready, 1)
                        if final:
                            dve.wait_ge(v_ready, s + 1)
                            dve.wait_ge(x_loaded[r], count_of(s, r, K))
                            if live(s - 4):
                                dve.wait_ge(stored[r], count_of(s - 4, r, K))
                            nc.vector.scalar_tensor_tensor(out=flat(res[:, r, :, :]), in0=flat(v[:, p, :, :]), scalar=0.0,
                                                           in1=flat(xs[:, r, :, :]), op0=ALU.max,
                                                           op1=ALU.add).then_inc(res_ready, 1)
                run_pipeline(dve, sh, step, -2, S, K)

            @block.scalar
            def _(act):
                def step(s, p):
                    r1, r0, q = (p + 1) % K, (p - 1) % K, (p + 1) % 2
                    if live(s + 5):
                        if live(s + 1):
                            act.wait_ge(gath_loaded[r1], count_of(s + 1, r1, K) * W)
                        nc.scalar.activation(ix[:, r1, :], c["idx"][:, ds((s + 5) * W, W)], ACT.Copy).then_inc(ix_ready, 1)
                    if live(s + 1):
                        act.wait_ge(t_done, s + 2)
                        if live(s - 1):
                            act.wait_ge(z_done, s)
                        nc.scalar.activation(st_hi[:, q, :], psT[q][:, :], ACT.Copy).then_inc(t_hi, 1)
                    if live(s - 1) and not final:
                        act.wait_ge(v_ready, s)
                        if live(s - 5):
                            act.wait_ge(stored[r0], count_of(s - 5, r0, K))
                        for t in range(T):
                            ins = nc.scalar.activation(res[:, r0, t, :], v[:, q, t, :], ACT.Relu,
                                                       scale=c["rsdeg"][:, ds((s - 1) * T + t, 1)])
                        ins.then_inc(res_ready, 1)
                run_pipeline(act, sh, step, -5, S, K)

            @block.tensor
            def _(pe):
                def step(s, p):
                    r1, p, q = (p + 1) % K, p % 2, (p + 1) % 2
                    if live(s + 1):
                        pe.wait_ge(own_loaded[r1], count_of(s + 1, r1, K))
                        pe.wait_ge(gath_loaded[r1], count_of(s + 1, r1, K) * W)
                        pe.wait_ge(hot_ready, s + 2)
                        if live(s - 1):
                            pe.wait_ge(t_lo, s)
                        for t in range(T):
                            nc.tensor.matmul(psT[q][:, t * P:(t + 1) * P], own[:, r1, t, :], c["ident"][:, :],
                                             is_transpose=True, start=t == 0, stop=False)
                        for w in range(W):
                            ins = nc.tensor.matmul(windows(psT[q][:, :])[:, :, W0[w]:W0[w] + WP[w]], gat[:, r1, w, :],
                                                   hot[:, q, w, :, 0:WP[w]], start=False, stop=w == W - 1)
                        ins.then_inc(t_done, 1)
                    if live(s):
                        pe.wait_ge(t_lo, s + 1)
                        if live(s - 2):
                            pe.wait_ge(v_ready, s - 1)
                        for t in range(T):
                            ins = product(nc, psZ[p][:, t * D:(t + 1) * D], st_hi[:, p, t * P:(t + 1) * P],
                                          st_lo[:, p, t * P:(t + 1) * P], *weight(c, w_name, 0), t == 0, t == T - 1)
                        ins.then_inc(z_done, 1)
                run_pipeline(pe, sh, step, -1, S, K)


_INS = ['x', 'src', 'dst', 'L0_gnn_W1a', 'L0_gnn_b1a', 'L0_gnn_W1b', 'L0_gnn_b1b', 'L0_gnn_W2a', 'L0_gnn_b2a',
        'L0_gnn_W2b', 'L0_gnn_b2b', 'L1_gnn_W1', 'L1_gnn_b1', 'L1_gnn_W2', 'L1_gnn_b2']


def kernel(**inputs):
    import numpy as _np
    import concourse.bacc as _bacc
    from concourse import mybir as _mybir
    from concourse.bass_utils import run_bass_kernel_spmd as _run

    nc = _bacc.Bacc("TRN2", target_bir_lowering=False, num_devices=1)
    arrays, args = {}, []
    for name in _INS:
        a = _np.ascontiguousarray(inputs[name])
        arrays[f"in_{name}_dram"] = a
        args.append(nc.dram_tensor(f"in_{name}_dram", a.shape, _mybir.dt.from_np(a.dtype), kind="ExternalInput").ap())
    out = nc.dram_tensor("out_0_dram", inputs["x"].shape, _mybir.dt.float32, kind="ExternalOutput").ap()
    graph_kernel(nc, *args, out)
    r = _run(nc, [arrays], core_ids=[0])
    return r.results[0]["out_0_dram"]
```
